# Optimizing a Trainium2 kernel written in Bass

```python
import numpy as np
import jax
import jax.numpy as jnp

def _softmax(x, axis=-1):
    return jax.nn.softmax(x, axis=axis)

def _gelu(x):
    return jax.nn.gelu(x, approximate=True)

def _silu(x):
    return jax.nn.silu(x)

def _sigmoid(x):
    return jax.nn.sigmoid(x)

def _layernorm(x, axis=-1, eps=1e-05):
    m = jnp.mean(x, axis=axis, keepdims=True)
    v = jnp.var(x, axis=axis, keepdims=True)
    return (x - m) / jnp.sqrt(v + eps)

def _scatter_add(tgt, idx, src, axis=0):
    return tgt.at[idx].add(src)

def _segment_sum(src, seg, n):
    return jax.ops.segment_sum(src, seg, n)
kernel_name = 'mk_gnn_preln_d2_gnn_r8_4a794c'

def setup_inputs(seed: int=0):
    np.random.seed(seed)
    _w = jnp.asarray

    def _rec_inputs():
        import jax
        import jax.numpy as jnp
        _gk = jax.random.key(seed)
        x = -0.0003713 + 1 * jax.random.normal(jax.random.fold_in(_gk, 1), (12500, 256), jnp.float32)
        src = jax.random.randint(jax.random.fold_in(_gk, 2), (200000,), 0, 12500, jnp.int32)
        dst = jnp.minimum((12500 * jax.random.uniform(jax.random.fold_in(_gk, 3), (200000,)) ** 2.0).astype(jnp.int32), 99999)
        _o = jnp.argsort(dst, stable=True)
        src = src[_o]
        dst = dst[_o]
        edge_weight = jax.random.uniform(jax.random.fold_in(_gk, 13), (200000,), jnp.float32, 0.0, 1)
        return (x, src, dst, edge_weight)
    x, src, dst, edge_weight = _rec_inputs()

    def _L0_gnn_setup():
        import jax, jax.numpy as jnp
        import numpy as np
        HEAD = 8
        D = 128
        GIN = 256
        GOUT = 256
        N = 6250
        E = 100000

        def gt_layer(edge_index, embeds, qT, kT, vT, ln_s, ln_b):
            rows, cols = (edge_index[0], edge_index[1])
            n, d = embeds.shape
            hd = d // HEAD
            rowE = embeds[rows]
            colE = embeds[cols]
            q = (rowE @ qT).reshape(-1, HEAD, hd)
            k = (colE @ kT).reshape(-1, HEAD, hd)
            v = (colE @ vT).reshape(-1, HEAD, hd)
            att = jnp.clip(jnp.einsum('ehd,ehd->eh', q, k), -10.0, 10.0)
            expAtt = jnp.exp(att)
            attNorm = jax.ops.segment_sum(expAtt, rows, num_segments=n)[rows]
            att = expAtt / (attNorm + 1e-08)
            res = (att[..., None] * v).reshape(-1, d)
            agg = jax.ops.segment_sum(res, rows, num_segments=n)
            out = agg + embeds
            mu = jnp.mean(out, axis=-1, keepdims=True)
            var = jnp.mean((out - mu) ** 2, axis=-1, keepdims=True)
            return (out - mu) / jnp.sqrt(var + 1e-06) * ln_s + ln_b
        key = jax.random.key(seed)
        ks = jax.random.split(key, 16)

        def xavier(k, shape):
            lim = np.sqrt(6.0 / (shape[0] + shape[1]))
            return jax.random.uniform(k, shape, jnp.float32, -lim, lim)
        inp = {'x': jax.random.normal(ks[0], (N, GIN), jnp.float32), 'edge_index': jax.random.randint(ks[1], (2, E), 0, N, jnp.int64), 'W_P_w': xavier(ks[2], (GIN, D)), 'W_P_b': jnp.zeros((D,), jnp.float32), 'W_pos': jax.random.uniform(ks[3], (1, D), jnp.float32, -0.02, 0.02), 'q1': xavier(ks[4], (D, D)), 'k1': xavier(ks[5], (D, D)), 'v1': xavier(ks[6], (D, D)), 'ln1_s': jnp.ones((D,), jnp.float32), 'ln1_b': jnp.zeros((D,), jnp.float32), 'q2': xavier(ks[7], (D, D)), 'k2': xavier(ks[8], (D, D)), 'v2': xavier(ks[9], (D, D)), 'ln2_s': jnp.ones((D,), jnp.float32), 'ln2_b': jnp.zeros((D,), jnp.float32), 'inv_w': xavier(ks[10], (D, GOUT)), 'inv_b': jnp.zeros((GOUT,), jnp.float32)}
        return inp
    _L0_gnn_all = _L0_gnn_setup()
    _L0_gnn_in = {k: v for k, v in _L0_gnn_all.items() if k in ('W_P_w', 'W_P_b', 'W_pos', 'q1', 'k1', 'v1', 'ln1_s', 'ln1_b', 'q2', 'k2', 'v2', 'ln2_s', 'ln2_b', 'inv_w', 'inv_b')}
    del _L0_gnn_all

    def _L1_gnn_setup():
        import jax, jax.numpy as jnp
        import numpy as np
        N_NODES = 12500
        N_EDGES = 400000
        D_IN = 256
        D_OUT = 256
        key = jax.random.key(seed)
        k1, k2, k3, k4, k5, k6 = jax.random.split(key, 6)
        x = jax.random.normal(k1, (N_NODES, D_IN), dtype=jnp.float32)
        edge_src = jax.random.randint(k2, (N_EDGES,), 0, N_NODES, dtype=jnp.int64)
        edge_dst = jax.random.randint(k3, (N_EDGES,), 0, N_NODES, dtype=jnp.int64)
        adj_vals = jax.random.uniform(k4, (N_EDGES,), dtype=jnp.float32)
        bound = 2.0 * np.sqrt(6.0 / (D_IN + D_OUT))
        w_nbr = jax.random.uniform(k5, (D_IN, D_OUT), dtype=jnp.float32, minval=-bound, maxval=bound)
        w_own = jax.random.uniform(k6, (D_IN, D_OUT), dtype=jnp.float32, minval=-bound, maxval=bound)
        bias = jnp.zeros((D_OUT,), dtype=jnp.float32)
        return {'x': x, 'edge_src': edge_src, 'edge_dst': edge_dst, 'adj_vals': adj_vals, 'w_nbr': w_nbr, 'w_own': w_own, 'bias': bias}
    _L1_gnn_all = _L1_gnn_setup()
    _L1_gnn_in = {k: v for k, v in _L1_gnn_all.items() if k in ('w_nbr', 'w_own', 'bias')}
    del _L1_gnn_all
    return {'x': x, 'src': src, 'dst': dst, 'edge_weight': edge_weight, 'L0_gnn_W_P_w': _L0_gnn_in['W_P_w'], 'L0_gnn_W_P_b': _L0_gnn_in['W_P_b'], 'L0_gnn_W_pos': _L0_gnn_in['W_pos'], 'L0_gnn_q1': _L0_gnn_in['q1'], 'L0_gnn_k1': _L0_gnn_in['k1'], 'L0_gnn_v1': _L0_gnn_in['v1'], 'L0_gnn_ln1_s': _L0_gnn_in['ln1_s'], 'L0_gnn_ln1_b': _L0_gnn_in['ln1_b'], 'L0_gnn_q2': _L0_gnn_in['q2'], 'L0_gnn_k2': _L0_gnn_in['k2'], 'L0_gnn_v2': _L0_gnn_in['v2'], 'L0_gnn_ln2_s': _L0_gnn_in['ln2_s'], 'L0_gnn_ln2_b': _L0_gnn_in['ln2_b'], 'L0_gnn_inv_w': _L0_gnn_in['inv_w'], 'L0_gnn_inv_b': _L0_gnn_in['inv_b'], 'L1_gnn_w_nbr': _L1_gnn_in['w_nbr'], 'L1_gnn_w_own': _L1_gnn_in['w_own'], 'L1_gnn_bias': _L1_gnn_in['bias']}

def reference(x, src, dst, edge_weight, L0_gnn_W_P_w, L0_gnn_W_P_b, L0_gnn_W_pos, L0_gnn_q1, L0_gnn_k1, L0_gnn_v1, L0_gnn_ln1_s, L0_gnn_ln1_b, L0_gnn_q2, L0_gnn_k2, L0_gnn_v2, L0_gnn_ln2_s, L0_gnn_ln2_b, L0_gnn_inv_w, L0_gnn_inv_b, L1_gnn_w_nbr, L1_gnn_w_own, L1_gnn_bias):
    import jax
    import jax.numpy as jnp

    def _L0_gnn_ref(x, edge_index, W_P_w, W_P_b, W_pos, q1, k1, v1, ln1_s, ln1_b, q2, k2, v2, ln2_s, ln2_b, inv_w, inv_b):
        import jax, jax.numpy as jnp
        import numpy as np
        HEAD = 8
        D = 128
        GIN = 256
        GOUT = 256
        N = 6250
        E = 100000

        def gt_layer(edge_index, embeds, qT, kT, vT, ln_s, ln_b):
            rows, cols = (edge_index[0], edge_index[1])
            n, d = embeds.shape
            hd = d // HEAD
            rowE = embeds[rows]
            colE = embeds[cols]
            q = (rowE @ qT).reshape(-1, HEAD, hd)
            k = (colE @ kT).reshape(-1, HEAD, hd)
            v = (colE @ vT).reshape(-1, HEAD, hd)
            att = jnp.clip(jnp.einsum('ehd,ehd->eh', q, k), -10.0, 10.0)
            expAtt = jnp.exp(att)
            attNorm = jax.ops.segment_sum(expAtt, rows, num_segments=n)[rows]
            att = expAtt / (attNorm + 1e-08)
            res = (att[..., None] * v).reshape(-1, d)
            agg = jax.ops.segment_sum(res, rows, num_segments=n)
            out = agg + embeds
            mu = jnp.mean(out, axis=-1, keepdims=True)
            var = jnp.mean((out - mu) ** 2, axis=-1, keepdims=True)
            return (out - mu) / jnp.sqrt(var + 1e-06) * ln_s + ln_b
        z = x @ W_P_w + W_P_b
        embeds = z + W_pos
        embeds = gt_layer(edge_index, embeds, q1, k1, v1, ln1_s, ln1_b)
        embeds = gt_layer(edge_index, embeds, q2, k2, v2, ln2_s, ln2_b)
        return embeds @ inv_w + inv_b

    def _L1_gnn_ref(x, edge_src, edge_dst, adj_vals, w_nbr, w_own, bias):
        import jax, jax.numpy as jnp
        import numpy as np
        N_NODES = 12500
        N_EDGES = 400000
        D_IN = 256
        D_OUT = 256
        h = x @ w_nbr
        msgs = adj_vals[:, None] * h[edge_src]
        agg = jax.ops.segment_sum(msgs, edge_dst, num_segments=x.shape[0])
        return agg + x @ w_own + bias
    edge_index = jnp.stack([src, dst])
    h = jnp.maximum(_layernorm(x, axis=-1), 0.0)
    x = x + _L0_gnn_ref(h, edge_index, L0_gnn_W_P_w, L0_gnn_W_P_b, L0_gnn_W_pos, L0_gnn_q1, L0_gnn_k1, L0_gnn_v1, L0_gnn_ln1_s, L0_gnn_ln1_b, L0_gnn_q2, L0_gnn_k2, L0_gnn_v2, L0_gnn_ln2_s, L0_gnn_ln2_b, L0_gnn_inv_w, L0_gnn_inv_b)
    h = jnp.maximum(_layernorm(x, axis=-1), 0.0)
    x = x + _L1_gnn_ref(h, src, dst, edge_weight, L1_gnn_w_nbr, L1_gnn_w_own, L1_gnn_bias)
    return x

_drawn_inputs = setup_inputs


def setup_inputs(seed=0):
    import zlib

    import numpy as np

    out = dict(_drawn_inputs(seed))
    spreads = {'L0_gnn_W_P_b': (0.0, 0.1),
     'L0_gnn_ln1_s': (1.0, 0.2),
     'L0_gnn_ln1_b': (0.0, 0.1),
     'L0_gnn_ln2_s': (1.0, 0.2),
     'L0_gnn_ln2_b': (0.0, 0.1),
     'L0_gnn_inv_b': (0.0, 0.1),
     'L1_gnn_bias': (0.0, 0.8)}
    factors = {'L0_gnn_W_pos': 3.412}
    for name, (base, spread) in spreads.items():
        noise = np.random.default_rng([zlib.crc32(name.encode()), seed]).standard_normal(out[name].shape)
        drawn = base * np.exp(spread * noise) if base else spread * noise
        out[name] = jnp.asarray(drawn.astype(out[name].dtype))
    for name, factor in factors.items():
        out[name] = (out[name] * factor).astype(out[name].dtype)
    return out
```

```python
import concourse.bass as bass
from concourse import mybir
from contextlib import ExitStack

P = 128
FP32 = mybir.dt.float32
BF16 = mybir.dt.bfloat16
I32 = mybir.dt.int32
U32 = mybir.dt.uint32
I16 = mybir.dt.int16
ALU = mybir.AluOpType
ACT = mybir.ActivationFunctionType
AX = mybir.AxisListType

BLOCKS = 14
TILES = 4
GROUPS = 20
RING = 5
HOTS = 4
CREDIT = 5
COLS = 8
COUNT_COLS = 4


def cdiv(a, b):
    return -(-a // b)


def done(n):
    return n + (1 + CREDIT)


def freed(n, slots):
    return n + (1 + CREDIT - slots)


def gnn_kernel(nc, x, src, dst, edge_weight, W_P_w, W_P_b, W_pos, q1, k1, v1, ln1_s, ln1_b,
               q2, k2, v2, ln2_s, ln2_b, inv_w, inv_b, w_nbr, w_own, bias, out):
    N, F = x.shape
    E = src.shape[0]
    D = q1.shape[0]
    H = 8
    HD = D // H
    MSG = D + H
    NB = cdiv(N, P)
    LAST = N - (NB - 1) * P
    KB = NB + 1
    C = cdiv(cdiv(E, P), 2 * COLS) * 2 * COLS
    NT = cdiv(cdiv(C * P + KB * (P - 1), P), TILES * GROUPS) * TILES * GROUPS
    GRID = cdiv(NT, P)
    NODE_STEPS = NB // BLOCKS
    EDGE_STEPS = NT // (TILES * GROUPS)
    EPS = 1e-5
    assert NB % BLOCKS == 0 and D == P and F == 2 * P

    ctx = ExitStack()
    with ctx:
        def sb(name, shape, dt=FP32):
            return ctx.enter_context(nc.sbuf_tensor(name, shape, dt))

        def sem(name):
            return ctx.enter_context(nc.semaphore(name))

        def dram(name, shape, dt=FP32):
            return nc.dram_tensor(name, shape, dt, kind="Internal").ap()

        kv_table = dram("kv_table", (NB * P, 2 * D))
        kv_table2 = dram("kv_table2", (NB * P, 2 * D))
        emb1_dram = dram("emb1_dram", (NB * P, D))
        emb2_dram = dram("emb2_dram", (NB * P, D))
        x1_dram = dram("x1_dram", (NB * P, F))
        h_table = dram("h_table", (NB * P, F))
        slots_src = dram("slots_src", (P * NT, 2))
        slots_dst = dram("slots_dst", (P * NT, 3))
        blocks_src = dram("blocks_src", (P * GRID,), I16)
        blocks_dst = dram("blocks_dst", (P * GRID,), I16)

        node_mem = sb("node_mem", [P, KB * max(MSG + D, F)])
        q_sb = node_mem[:, 0:KB * D].rearrange("p (b d) -> p b d", d=D)
        agg_sb = node_mem[:, KB * D:KB * (D + MSG)].rearrange("p (b d) -> p b d", d=MSG)
        conv_sb = node_mem[:, 0:KB * F].rearrange("p (b d) -> p b d", d=F)
        s0 = KB * D
        key_blk = node_mem[:, s0:s0 + C]
        rec_all = node_mem[:, s0 + C:s0 + 4 * C].rearrange("p (c w) -> p c w", w=3)
        key_int = node_mem[:, s0 + 4 * C:s0 + 5 * C].bitcast(I32)
        oth_int = node_mem[:, s0 + 5 * C:s0 + 6 * C].bitcast(I32)
        blk_int = node_mem[:, s0 + 6 * C:s0 + 7 * C].bitcast(I32)
        empty = node_mem[:, s0 + 5 * C:s0 + 5 * C + 3 * NT]
        assert 7 * C <= KB * MSG and 5 * C + 3 * NT <= KB * MSG

        slot_mem = sb("slot_mem", [P, NT * 3])
        slot_src = slot_mem[:, 0:NT * 2].rearrange("p (t w) -> p t w", w=2)
        slot_dst = slot_mem[:, :].rearrange("p (t w) -> p t w", w=3)
        gidx = sb("gidx", [P, NT], U32)
        blk_row = sb("blk_row", [1, P * GRID], I16)
        idx_ring = sb("idx_ring", [P, RING, TILES], U32)

        RINGW = RING * TILES * F
        GW = TILES * P
        work = sb("work", [P, BLOCKS * 3 * F])
        rows = work[:, 0:RINGW].rearrange("p (g t f) -> p g t f", g=RING, t=TILES)
        o = RINGW
        hot = work[:, o:o + HOTS * GW].rearrange("p (g t n) -> p g t n", g=HOTS, t=TILES)
        o += HOTS * GW
        hotT = work[:, o:o + 2 * GW].rearrange("p (g n) -> p g n", g=2)
        o += 2 * GW
        hot16 = work[:, o:o + GW].bitcast(BF16).rearrange("p (g t n) -> p g t n", g=2, t=TILES)
        o += GW
        prod = work[:, o:o + GW]
        o += GW
        msg = work[:, o:o + 2 * TILES * MSG].rearrange("p (g t m) -> p g t m", g=2, t=TILES)
        assert o + 2 * TILES * MSG <= BLOCKS * 3 * F
        x14 = work[:, 0:BLOCKS * F].rearrange("p (b f) -> p b f", f=F)
        o14 = work[:, BLOCKS * F:2 * BLOCKS * F].rearrange("p (b f) -> p b f", f=F)
        e14 = work[:, 2 * BLOCKS * F:BLOCKS * (2 * F + D)].rearrange("p (b f) -> p b f", f=D)
        c14 = work[:, 2 * BLOCKS * F:3 * BLOCKS * F].rearrange("p (b f) -> p b f", f=F)
        y14 = work[:, BLOCKS * (2 * F + D):BLOCKS * (2 * F + 2 * D)].rearrange("p (b f) -> p b f", f=D)

        hs = sb("hs", [P, 2, F])
        hsT = sb("hsT", [P, 2, 2 * F])
        eT = sb("eT", [P, 2, D])
        score = sb("score", [P, 2, TILES * H])

        wp = sb("wp", [P, 2, D])
        wqkv1 = sb("wqkv1", [P, 3 * D])
        wqkv2 = sb("wqkv2", [P, 3 * D])
        winv = sb("winv", [P, F])
        wn = sb("wn", [P, 2, F])
        wo = sb("wo", [P, 2, F])
        pbias = sb("pbias", [P, 2, D])
        lns = sb("lns", [P, 2, 2, D])
        invb = sb("invb", [P, F])
        cbias = sb("cbias", [P, F])

        st6 = sb("st6", [P, BLOCKS, 6])
        mv = sb("mv", [P, BLOCKS, 2])
        sd = sb("sd", [P, BLOCKS])
        rs = sb("rs", [P, BLOCKS])
        nb = sb("nb", [P, BLOCKS])
        rnorm = sb("rnorm", [P, BLOCKS, H])

        iota_n = sb("iota_n", [P, P])
        iota16 = sb("iota16", [P, P], BF16)
        ident = sb("ident", [P, P])
        ident16 = sb("ident16", [P, P], BF16)
        below = sb("below", [P, P])
        ones = sb("ones", [P, P])
        grid = sb("grid", [P, GRID])
        hot_cnt = sb("hot_cnt", [P, 2, COUNT_COLS, KB], BF16)
        cnt = sb("cnt", [P, KB])
        tot = sb("tot", [P, KB])
        tot_i = sb("tot_i", [P, KB], I32)
        ntile = sb("ntile", [P, KB])
        tend = sb("tend", [P, KB])
        nxt = sb("nxt", [P, KB])
        junk = sb("junk", [P, KB])
        blk_f = sb("blk_f", [P, GRID])
        blk_i = sb("blk_i", [P, GRID], I16)
        slot_f = sb("slot_f", [P, COLS])
        slot_i = sb("slot_i", [P, COLS], I32)
        lane_i = sb("lane_i", [P, COLS], I32)
        tile_i = sb("tile_i", [P, COLS], I32)
        tile_f = sb("tile_f", [P, COLS])
        lane_f = sb("lane_f", [P, COLS])
        pos_ring = sb("pos_ring", [P, 2, COLS], U32)
        rec_ring = sb("rec_ring", [P, 2, COLS, 3])

        pb = [ctx.enter_context(nc.psum_tensor(f"pb{n}", [P, 512], FP32)) for n in range(4)]
        pw = [ctx.enter_context(nc.psum_tensor(f"pw{n}", [P, 2, 512], FP32)) for n in range(2)]

        hotT_ps = [pb[n][:, 0:GW // 2].bitcast(BF16) for n in range(2)]

        def pw4(n):
            return pw[n][:, :, :].rearrange("p a (b c) -> p (a b) c", b=2)

        s_const = sem("s_const")
        s_id16 = sem("s_id16")
        s_past = sem("s_past")
        s_w = sem("s_w")
        NW = 21
        s_big = [sem(f"s_big{k}") for k in range(2)]

        def names(tag, *what):
            return {w: sem(f"{tag}_{w}") for w in what}

        sorts = [names(t, "keys", "in", "link", "hot", "add", "cnt", "sums", "empty_ms", "empty", "brow",
                       "row", "base", "chain", "conv", "pos", "rec", "out0", "out1", "loaded", "gidx")
                 for t in ("sort_src", "sort_dst")]
        node_sems = [
            names("n0", "x", "link", "st", "sqrt", "rs", "h", "hT_ps", "hT", "mm", "emb", "eT_ps", "eT", "qkv",
                  "q", "kv", "part", "out"),
            names("n1", "e", "link", "st", "sqrt", "eT_ps", "eT", "qkv", "q", "kv", "y", "used", "part", "out"),
            names("n2", "x", "e", "link", "st", "sqrt", "rs", "h", "eT_ps", "eT", "qkv", "q", "y", "used", "sum",
                  "part", "out"),
            names("n3", "c", "x", "e", "hT_ps", "eT", "q", "mm", "sum", "out")]
        s_idx = [sem(f"s_idx{r}") for r in range(RING)]
        s_rows = [sem(f"s_rows{r}") for r in range(RING)]

        def idx_in(which, i, g):
            return 16 * (i * (GROUPS // RING) + (g // RING + 1 + which * EDGE_STEPS * (GROUPS // RING)))

        def rows_in(which, i, g):
            return 16 * TILES * (i * (GROUPS // RING) + (g // RING + 1 + which * EDGE_STEPS * (GROUPS // RING)))

        edge_sems = [names(t, "hot", "hotT_ps", "hotT", "q", "prod", "score", "clip", "exp", "msg", "agg",
                           "add", "clear", "hot32") for t in ("e0", "e1")]
        edge_sems.append(names("e2", "hot", "agg", "add", "clear"))

        block = ctx.enter_context(nc.Block())

        def tile_blocks(engine, n):
            _, values = nc.values_load_multi_w_load_instructions(
                blk_row[0:1, bass.ds(n * TILES, TILES)], engines=[engine], min_val=0, max_val=KB - 1,
                skip_runtime_bounds_check_because="the sort caps each at the last block")
            return values

        def give_credit(eng, sems):
            for s in sems:
                eng.sem_inc(s, CREDIT)

        NODE_DVE = ("hT", "emb", "q", "sum")
        NODE_ACT = ("h", "eT", "kv")
        NODE_PE = ("hT_ps", "mm", "eT_ps", "qkv")
        EDGE_DVE = ("hot", "prod", "score", "clip", "msg", "add")
        EDGE_ACT = ("hot32", "hotT", "exp")
        EDGE_PE = ("hotT_ps", "q", "agg")

        @block.sync
        def _(sp):
            def row(v):
                return v.rearrange("(a n) -> a n", a=1) if len(v.shape) == 1 else v

            for ap, s in ((wp[:, :, :], W_P_w.rearrange("(k p) n -> p k n", p=P)),
                          (wn[:, :, :], w_nbr.rearrange("(k p) n -> p k n", p=P)),
                          (wo[:, :, :], w_own.rearrange("(k p) n -> p k n", p=P)),
                          (winv[:, :], inv_w),
                          (wqkv1[:, 0:D], q1), (wqkv1[:, D:2 * D], k1), (wqkv1[:, 2 * D:3 * D], v1),
                          (wqkv2[:, 0:D], q2), (wqkv2[:, D:2 * D], k2), (wqkv2[:, 2 * D:3 * D], v2)):
                sp.dma_start(ap, s).then_inc(s_w, 16)
            for ap, s in ((pbias[:, 0, :], W_P_b), (pbias[:, 1, :], W_pos),
                          (lns[:, 0, 0, :], ln1_s), (lns[:, 0, 1, :], ln1_b),
                          (lns[:, 1, 0, :], ln2_s), (lns[:, 1, 1, :], ln2_b),
                          (invb[:, :], inv_b), (cbias[:, :], bias)):
                w = row(s)
                sp.dma_start(ap, w.to_broadcast([P, w.shape[1]])).then_inc(s_w, 16)

            def load_lists(which):
                s = sorts[which]
                slots, to = ((slots_src, slot_src), (slots_dst, slot_dst))[which]
                sp.dma_start(to[:, :, :], slots.rearrange("(p t) w -> p t w", p=P)).then_inc(s["loaded"], 16)
                sp.dma_start(blk_row[:, :], (blocks_src, blocks_dst)[which].rearrange("(a n) -> a n", a=1))\
                    .then_inc(s["row"], 16)

            full, rest = E // C, E % C
            fold = full // 16 * 16
            for which, s in enumerate(sorts):
                key, oth = (src, dst) if which == 0 else (dst, src)
                sp.wait_ge(s["keys"], 1)
                for v, to in ((key, key_int), (oth, oth_int), (edge_weight, key_blk))[:2 + which]:
                    for a, b in ((0, fold), (fold, full)):
                        if b > a:
                            sp.dma_start(to[a:b, :], v[a * C:b * C].rearrange("(p c) -> p c", c=C)).then_inc(s["in"], 16)
                    if rest:
                        sp.dma_start(to[full:full + 1, 0:rest],
                                     v[full * C:E].rearrange("(p c) -> p c", p=1)).then_inc(s["in"], 16)
                slots, width = (slots_src, 2) if which == 0 else (slots_dst, 3)
                sp.wait_ge(s["empty_ms"], 1)
                sp.dma_start(slots.rearrange("(p t) w -> p (t w)", p=P), empty[:, 0:NT * width]).then_inc(s["empty"], 16)
                sp.wait_ge(s["brow"], 1)
                br = blocks_src if which == 0 else blocks_dst
                sp.dma_start(br.rearrange("(p c) -> p c", p=P), blk_i[:, :]).then_inc(s["row"], 16)
                sp.wait_ge(s["row"], 16)
                for par in range(2):
                    sp.wait_ge(s[f"out{par}"], 16 * COLS * (C // COLS // 2))
                if which == 0:
                    load_lists(0)

            def rows_of(table, i):
                return table[bass.ds(i * (BLOCKS * P), BLOCKS * P), :].rearrange("(b p) f -> p b f", p=P)

            def ragged(i, last):
                whole = BLOCKS - 1
                n = LAST if last else P
                return (whole, slice(0, P), bass.ds(i * (BLOCKS * P), whole * P)), \
                       (whole, slice(0, n), bass.ds(i * (BLOCKS * P) + whole * P, n))

            def load_x(i, last, s_in):
                (w, _, a), (_, lanes, b) = ragged(i, last)
                sp.dma_start(x14[:, 0:w, :], x[a, :].rearrange("(b p) f -> p b f", p=P)).then_inc(s_in, 16)
                sp.dma_start(x14[lanes, w, :], x[b, :]).then_inc(s_in, 16)

            def node_loop(step):
                if NODE_STEPS > 1:
                    with sp.Fori(0, NODE_STEPS - 1) as i:
                        step(i, False)
                step(NODE_STEPS - 1, True)

            sp.wait_ge(s_const, 9)

            def stage0(i, last):
                s = node_sems[0]
                load_x(i, last, s["x"])
                sp.wait_ge(s["emb"], done(i * BLOCKS + BLOCKS - 1))
                sp.dma_start(rows_of(emb1_dram, i), e14[:, :, :]).then_inc(s["out"], 16)
                sp.wait_ge(s["kv"], done(i * BLOCKS + BLOCKS - 1))
                sp.dma_start(rows_of(kv_table, i), o14[:, :, :]).then_inc(s["out"], 16)
                sp.wait_ge(s["out"], i * 32 + 32)
                sp.sem_inc(s_past, 1)
            node_loop(stage0)

            def gather_lists(which, slots_idx):
                s = edge_sems[which]
                free = "msg" if which < 2 else "agg"
                with sp.Fori(0, EDGE_STEPS) as i:
                    for g in range(GROUPS):
                        n = i * GROUPS + g
                        sp.wait_ge(s[free], freed(n, RING))
                        sp.dma_start(idx_ring[:, g % RING, :], slots_idx[:, bass.ds(n * TILES, TILES)])\
                            .then_inc(s_idx[g % RING], 16)

            sp.wait_ge(sorts[0]["gidx"], 1)
            gather_lists(0, gidx)
            sp.wait_ge(edge_sems[0]["add"], CREDIT + NT)

            def stage1(i, last):
                s = node_sems[1]
                sp.dma_start(e14[:, :, :], rows_of(emb1_dram, i)).then_inc(s["e"], 16)
                sp.wait_ge(s["y"], i + 1)
                sp.dma_start(rows_of(emb2_dram, i), e14[:, :, :]).then_inc(s["out"], 16)
                sp.wait_ge(s["kv"], done(i * BLOCKS + BLOCKS - 1))
                sp.dma_start(rows_of(kv_table2, i), o14[:, :, :]).then_inc(s["out"], 16)
                sp.wait_ge(s["q"], done(i * BLOCKS + BLOCKS - 1))
                sp.wait_ge(s["out"], i * 32 + 32)
                sp.sem_inc(s_past, 1)
            node_loop(stage1)

            gather_lists(1, gidx)
            sp.wait_ge(edge_sems[1]["add"], CREDIT + NT)

            load_lists(1)

            def stage2(i, last):
                s = node_sems[2]
                sp.dma_start(e14[:, :, :], rows_of(emb2_dram, i)).then_inc(s["e"], 16)
                load_x(i, last, s["x"])
                sp.wait_ge(s["sum"], done(i * BLOCKS + BLOCKS - 1))
                sp.dma_start(rows_of(x1_dram, i), o14[:, :, :]).then_inc(s["out"], 16)
                sp.wait_ge(s["h"], done(i * BLOCKS + BLOCKS - 1))
                sp.dma_start(rows_of(h_table, i), x14[:, :, :]).then_inc(s["out"], 16)
                sp.wait_ge(s["out"], i * 32 + 32)
                sp.sem_inc(s_past, 1)
            node_loop(stage2)

            sp.wait_ge(sorts[1]["gidx"], 1)
            gather_lists(2, gidx)
            sp.wait_ge(edge_sems[2]["add"], CREDIT + NT)

            def stage3(i, last):
                s = node_sems[3]
                sp.dma_start(x14[:, :, :], rows_of(h_table, i)).then_inc(s["x"], 16)
                sp.dma_start(o14[:, :, :], rows_of(x1_dram, i)).then_inc(s["e"], 16)
                sp.wait_ge(s["sum"], done(i * BLOCKS + BLOCKS - 1))
                (w, _, a), (_, lanes, b) = ragged(i, last)
                sp.dma_start(out[a, :].rearrange("(b p) f -> p b f", p=P), o14[:, 0:w, :]).then_inc(s["out"], 16)
                sp.dma_start(out[b, :], o14[lanes, w, :]).then_inc(s["out"], 16)
                sp.wait_ge(s["out"], i * 32 + 32)
                sp.sem_inc(s_past, 1)
            node_loop(stage3)

        @block.gpsimd
        def _(pool):
            pool.iota(iota_n[:, :], pattern=[[1, P]], base=0, channel_multiplier=0,
                      allow_small_or_imprecise_dtypes=True).then_inc(s_const, 1)
            pool.iota(grid[:, :], pattern=[[1, GRID]], base=0, channel_multiplier=GRID,
                      allow_small_or_imprecise_dtypes=True).then_inc(s_const, 1)
            pool.memset(ident[:, :], 0.0).then_inc(s_const, 1)
            pool.memset(ones[:, :], 1.0).then_inc(s_const, 1)
            pool.memset(below[:, :], 1.0).then_inc(s_const, 1)
            pool.wait_ge(s_const, 5)
            pool.affine_select(out=ident[:, :], in_=ident[:, :], compare_op=ALU.not_equal, fill=1.0,
                               base=0, pattern=[[-1, P]], channel_multiplier=1).then_inc(s_const, 1)
            pool.affine_select(out=below[:, :], in_=below[:, :], compare_op=ALU.is_gt, fill=0.0,
                               base=0, pattern=[[1, P]], channel_multiplier=-1).then_inc(s_const, 1)
            pool.memset(q_sb[:, NB, :], 0.0).then_inc(s_const, 1)
            pool.memset(work[:, :], 0.0).then_inc(s_const, 1)

            for which, s in enumerate(sorts):
                slots, width = (slots_src, 2) if which == 0 else (slots_dst, 3)
                pool.wait_ge(s["empty"], 16)
                with pool.Fori(0, C // COLS // 2) as i:
                    for par in range(2):
                        n = i * 2 + par
                        pool.wait_ge(s["pos"], done(n))
                        pool.wait_ge(s["rec"], done(n))
                        pool.sem_inc(s_past, 1)
                        for u in range(COLS):
                            pool.indirect_dma_start(
                                out=slots[:, :], out_offset=bass.IndirectOffsetOnAxis(ap=pos_ring[:, par, u:u + 1], axis=0),
                                in_=rec_ring[:, par, u, 0:width], in_offset=None).then_inc(s[f"out{par}"], 16)

            def gathers(which, table):
                with pool.Fori(0, EDGE_STEPS) as i:
                    for g in range(GROUPS):
                        r = g % RING
                        pool.wait_ge(s_idx[r], idx_in(which, i, g))
                        pool.sem_inc(s_past, 1)
                        for u in range(TILES):
                            pool.indirect_dma_start(
                                out=rows[:, r, u, :], out_offset=None, in_=table[:, :],
                                in_offset=bass.IndirectOffsetOnAxis(ap=idx_ring[:, r, u:u + 1], axis=0)).then_inc(s_rows[r], 16)

            for which in range(3):
                s = edge_sems[which]
                if which == 0:
                    for par in range(2):
                        pool.wait_ge(sorts[1][f"out{par}"], 16 * COLS * (C // COLS // 2))
                else:
                    pool.wait_ge(node_sems[which]["used"], NODE_STEPS)
                pool.memset((agg_sb if which < 2 else conv_sb)[:, :, :], 0.0).then_inc(s["clear"], 1)
                pool.wait_ge(node_sems[which]["out"], 32 * NODE_STEPS)
                gathers(which, (kv_table, kv_table2, h_table)[which])

        @block.scalar
        def _(act):
            for s in node_sems:
                give_credit(act, [s[k] for k in NODE_ACT if k in s])
            for s in edge_sems:
                give_credit(act, [s[k] for k in EDGE_ACT if k in s])
            for s in sorts:
                give_credit(act, [s["rec"]])
            act.wait_ge(s_const, 7)
            act.copy(ident16[:, :], ident[:, :]).then_inc(s_id16, 1)
            act.copy(iota16[:, :], iota_n[:, :]).then_inc(s_id16, 1)

            for which, s in enumerate(sorts):
                act.wait_ge(s["base"], 1)

                def records(i):
                    for par in range(2):
                        n = i * 2 + par
                        if not isinstance(i, int):
                            act.wait_ge(s[f"out{par}"], i * (16 * COLS))
                        act.copy(rec_ring[:, par, :, :], rec_all[:, bass.ds(n * COLS, COLS), :]).then_inc(s["rec"], 1)
                records(0)
                with act.Fori(1, C // COLS // 2) as i:
                    records(i)
                if which == 0:
                    act.wait_ge(s["loaded"], 16)
                    act.copy(gidx[:, :], slot_src[:, :, 1]).then_inc(s["gidx"], 1)

            s = node_sems[0]
            act.wait_ge(sorts[0]["gidx"], 1)
            with act.Fori(0, NODE_STEPS) as i:
                act.wait_ge(s["st"], i + 1)
                act.activation(sd[:, :], sd[:, :], ACT.Sqrt).then_inc(s["sqrt"], 1)
                act.wait_ge(s["rs"], i + 1)
                for t in range(BLOCKS + 4):
                    j = t
                    if j < BLOCKS:
                        n = i * BLOCKS + j
                        act.wait_ge(s["hT_ps"], freed(n, 2))
                        act.activation(hs[:, j % 2, :], x14[:, j, :], ACT.Relu, bias=nb[:, j:j + 1],
                                       scale=rs[:, j:j + 1]).then_inc(s["h"], 1)
                    j = t - 3
                    if 0 <= j < BLOCKS:
                        n = i * BLOCKS + j
                        act.wait_ge(s["eT_ps"], done(n))
                        act.wait_ge(s["qkv"], freed(n, 2))
                        act.copy(eT[:, j % 2, :], pw[0][:, j % 2, 0:D]).then_inc(s["eT"], 1)
                    j = t - 4
                    if 0 <= j < BLOCKS:
                        n = i * BLOCKS + j
                        act.wait_ge(s["qkv"], done(n))
                        
                        act.copy(o14[:, j, :], pw[1][:, j % 2, D:3 * D]).then_inc(s["kv"], 1)

            def attention_act(which):
                s = edge_sems[which]
                with act.Fori(0, EDGE_STEPS) as i:
                    for t in range(GROUPS + 2):
                        g = t - 2
                        if 0 <= g < GROUPS:
                            n = i * GROUPS + g
                            act.wait_ge(s["clip"], done(n))
                            act.activation(msg[:, g % 2, :, D:MSG],
                                           score[:, g % 2, :].rearrange("p (t h) -> p t h", h=H), ACT.Exp)\
                                .then_inc(s["exp"], 1)
                        g = t
                        if g < GROUPS:
                            n = i * GROUPS + g
                            act.wait_ge(s["hot"], done(n))
                            act.copy(hot[:, g % HOTS, :, :], hot16[:, g % 2, :, :]).then_inc(s["hot32"], 1)
                            act.wait_ge(s["hotT_ps"], done(n))
                            if g >= 2:
                                act.wait_ge(s["q"], done(n - 2))
                            act.copy(hotT[:, g % 2, :], hotT_ps[g % 2]).then_inc(s["hotT"], 1)

            attention_act(0)
            s = node_sems[1]
            with act.Fori(0, NODE_STEPS) as i:
                act.wait_ge(s["st"], i + 1)
                act.activation(sd[:, :], sd[:, :], ACT.Sqrt).then_inc(s["sqrt"], 1)
                for t in range(BLOCKS + 1):
                    j = t
                    if j < BLOCKS:
                        n = i * BLOCKS + j
                        act.wait_ge(s["eT_ps"], done(n))
                        act.wait_ge(s["qkv"], freed(n, 2))
                        act.copy(eT[:, j % 2, :], pw[0][:, j % 2, 0:D]).then_inc(s["eT"], 1)
                    j = t - 1
                    if 0 <= j < BLOCKS:
                        n = i * BLOCKS + j
                        act.wait_ge(s["qkv"], done(n))
                        act.copy(o14[:, j, :], pw[1][:, j % 2, D:3 * D]).then_inc(s["kv"], 1)
            attention_act(1)
            act.wait_ge(sorts[1]["loaded"], 16)
            act.wait_ge(edge_sems[1]["add"], CREDIT + NT)
            act.copy(gidx[:, :], slot_dst[:, :, 1]).then_inc(sorts[1]["gidx"], 1)
            s = node_sems[2]
            with act.Fori(0, NODE_STEPS) as i:
                act.wait_ge(s["st"], 2 * i + 1)
                act.activation(sd[:, :], sd[:, :], ACT.Sqrt).then_inc(s["sqrt"], 1)
                for j in range(BLOCKS):
                    n = i * BLOCKS + j
                    act.wait_ge(s["eT_ps"], done(n))
                    act.wait_ge(s["qkv"], freed(n, 2))
                    act.copy(eT[:, j % 2, :], pw[0][:, j % 2, 0:D]).then_inc(s["eT"], 1)
                act.wait_ge(s["st"], 2 * i + 2)
                act.activation(sd[:, :], sd[:, :], ACT.Sqrt).then_inc(s["sqrt"], 1)
                act.wait_ge(s["rs"], i + 1)
                for j in range(BLOCKS):
                    n = i * BLOCKS + j
                    act.activation(x14[:, j, :], o14[:, j, :], ACT.Relu, bias=nb[:, j:j + 1],
                                   scale=rs[:, j:j + 1]).then_inc(s["h"], 1)
            s = node_sems[3]
            act.wait_ge(edge_sems[2]["add"], CREDIT + NT)
            with act.Fori(0, NODE_STEPS) as i:
                act.wait_ge(s["hT_ps"], i * BLOCKS + CREDIT)
                act.copy(c14[:, :, :], conv_sb[:, bass.ds(i * BLOCKS, BLOCKS), :]).then_inc(s["c"], 1)
                for j in range(BLOCKS):
                    n = i * BLOCKS + j
                    act.wait_ge(s["hT_ps"], done(n))
                    act.wait_ge(s["mm"], freed(n, 2))
                    act.copy(hsT[:, j % 2, :], pb[j % 2][:, :]).then_inc(s["eT"], 1)

        @block.tensor
        def _(pe):
            for s in node_sems:
                give_credit(pe, [s[k] for k in NODE_PE if k in s])
            for s in edge_sems:
                give_credit(pe, [s[k] for k in EDGE_PE if k in s])
            for s in sorts:
                give_credit(pe, [s["add"]])
            pe.wait_ge(s_const, 7)
            pe.wait_ge(s_id16, 1)
            pe.wait_ge(s_w, 16 * 18)

            for which, s in enumerate(sorts):
                W = COUNT_COLS * KB
                steps = C // COUNT_COLS
                def count(n, par, first, last):
                    pe.wait_ge(s["hot"], done(n))
                    nc.tensor.matmul(pb[0][:, 0:W], ident16[:, :], hot_cnt[:, par, :, :].rearrange("p c b -> p (c b)"),
                                     start=first, stop=last).then_inc(s["add"], 1)
                count(0, 0, True, False)
                count(1, 1, False, False)
                if steps > 4:
                    with pe.Fori(1, steps // 2 - 1) as i:
                        for par in range(2):
                            count(i * 2 + par, par, False, False)
                count(steps - 2, 0, False, False)
                count(steps - 1, 1, False, True)
                pe.wait_ge(s["cnt"], 1)
                nc.tensor.matmul(pb[1][:, 0:KB], below[:, :], cnt[:, :], start=True, stop=True)
                nc.tensor.matmul(pb[2][:, 0:KB], ones[:, :], cnt[:, :], start=True, stop=True).then_inc(s["sums"], 1)

            def qkv_steps(i, s, w, t):
                j = t
                if 0 <= j < BLOCKS:
                    n = i * BLOCKS + j
                    pe.wait_ge(s["eT"], freed(n, 2))
                    nc.tensor.transpose(pw[0][:, j % 2, 0:D], e14[:, j, :], ident[:, :]).then_inc(s["eT_ps"], 1)
                j = t - 1
                if 0 <= j < BLOCKS:
                    n = i * BLOCKS + j
                    pe.wait_ge(s["eT"], done(n))
                    pe.wait_ge(s["q"], freed(n, 2))
                    pe.wait_ge(s["kv"], freed(n, 2))
                    nc.tensor.matmul(pw[1][:, j % 2, 0:3 * D], eT[:, j % 2, :], w[:, :], start=True, stop=True)\
                        .then_inc(s["qkv"], 1)

            s = node_sems[0]
            with pe.Fori(0, NODE_STEPS) as i:
                for t in range(BLOCKS + 4):
                    j = t
                    if j < BLOCKS:
                        n = i * BLOCKS + j
                        pe.wait_ge(s["h"], done(n))
                        pe.wait_ge(s["hT"], freed(n, 2))
                        nc.tensor.transpose(pb[j % 2][:, 0:P], hs[:, j % 2, 0:P], ident[:, :])
                        nc.tensor.transpose(pb[j % 2][:, P:2 * P], hs[:, j % 2, P:2 * P], ident[:, :])\
                            .then_inc(s["hT_ps"], 1)
                    j = t - 1
                    if 0 <= j < BLOCKS:
                        n = i * BLOCKS + j
                        pe.wait_ge(s["hT"], done(n))
                        pe.wait_ge(s["emb"], freed(n, 2))
                        nc.tensor.matmul(pb[2 + j % 2][:, 0:D], hsT[:, j % 2, 0:P], wp[:, 0, :], start=True, stop=False)
                        nc.tensor.matmul(pb[2 + j % 2][:, 0:D], hsT[:, j % 2, P:2 * P], wp[:, 1, :], start=False,
                                         stop=True).then_inc(s["mm"], 1)
                    if 0 <= t - 2 < BLOCKS:
                        pe.wait_ge(s["emb"], done(i * BLOCKS + t - 2))
                    qkv_steps(i, s, wqkv1, t - 2)

            def attention_pe(which):
                s = edge_sems[which]
                pe.wait_ge(s["clear"], 1)
                with pe.Fori(0, EDGE_STEPS) as i:
                    for t in range(GROUPS + 3):
                        if t < GROUPS:
                            g = t
                            n = i * GROUPS + g
                            pe.wait_ge(s["hot"], done(n))
                            for u in range(TILES):
                                last = nc.tensor.transpose(hotT_ps[g % 2][:, u * P:(u + 1) * P],
                                                           hot16[:, g % 2, u, :], ident16[:, :])
                            last.then_inc(s["hotT_ps"], 1)
                        g = t - 3
                        if g >= 0:
                            n = i * GROUPS + g
                            pe.wait_ge(s["msg"], done(n))
                            for u in range(TILES):
                                last = nc.tensor.matmul(pw4(g % 2)[:, u, 0:MSG], hot[:, g % HOTS, u, :],
                                                        msg[:, g % 2, u, :], start=True, stop=True)
                            last.then_inc(s["agg"], 1)
                        if t < GROUPS:
                            g = t
                            n = i * GROUPS + g
                            blks = tile_blocks(mybir.EngineType.PE, n)
                            pe.wait_ge(s["hotT"], done(n))
                            if g >= 2:
                                pe.wait_ge(s["prod"], done(n - 2))
                            for u in range(TILES):
                                last = nc.tensor.matmul(pb[2 + g % 2][:, u * P:(u + 1) * P],
                                                        hotT[:, g % 2, u * P:(u + 1) * P],
                                                        q_sb[:, bass.ds(blks[u], 1), :], start=True, stop=True)
                            last.then_inc(s["q"], 1)

            pe.wait_ge(sorts[0]["row"], 32)
            attention_pe(0)
            s = node_sems[1]
            with pe.Fori(0, NODE_STEPS) as i:
                pe.wait_ge(s["y"], i + 1)
                for t in range(BLOCKS + 1):
                    qkv_steps(i, s, wqkv2, t)
            attention_pe(1)
            s = node_sems[2]
            with pe.Fori(0, NODE_STEPS) as i:
                pe.wait_ge(s["y"], i + 1)
                for t in range(BLOCKS + 1):
                    j = t
                    if j < BLOCKS:
                        n = i * BLOCKS + j
                        pe.wait_ge(s["eT"], freed(n, 2))
                        nc.tensor.transpose(pw[0][:, j % 2, 0:D], e14[:, j, :], ident[:, :]).then_inc(s["eT_ps"], 1)
                    j = t - 1
                    if j >= 0:
                        n = i * BLOCKS + j
                        pe.wait_ge(s["eT"], done(n))
                        pe.wait_ge(s["sum"], freed(n, 2))
                        nc.tensor.matmul(pw[1][:, j % 2, 0:F], eT[:, j % 2, :], winv[:, :], start=True, stop=True)\
                            .then_inc(s["qkv"], 1)
            s = edge_sems[2]
            pe.wait_ge(s["clear"], 1)
            with pe.Fori(0, EDGE_STEPS) as i:
                for g in range(GROUPS):
                    n = i * GROUPS + g
                    pe.wait_ge(s["hot"], done(n))
                    pe.wait_ge(s_rows[g % RING], rows_in(2, i, g))
                    if g >= 2:
                        pe.wait_ge(s["add"], n * TILES + (CREDIT - TILES))
                    for u in range(TILES):
                        last = nc.tensor.matmul(pw4(g % 2)[:, u, :], hot[:, g % HOTS, u, :], rows[:, g % RING, u, :],
                                                start=True, stop=True)
                    last.then_inc(s["agg"], 1)
            s = node_sems[3]
            with pe.Fori(0, NODE_STEPS) as i:
                pe.wait_ge(s["x"], (i + 1) * 16)
                pe.wait_ge(s["c"], i + 1)
                for t in range(BLOCKS + 1):
                    j = t
                    if j < BLOCKS:
                        n = i * BLOCKS + j
                        pe.wait_ge(s["eT"], freed(n, 2))
                        for k in range(2):
                            nc.tensor.transpose(pb[j % 2][:, k * P:(k + 1) * P],
                                                c14[:, j, k * P:(k + 1) * P], ident[:, :])
                        for k in range(2):
                            last = nc.tensor.transpose(pb[j % 2][:, (2 + k) * P:(3 + k) * P],
                                                       x14[:, j, k * P:(k + 1) * P], ident[:, :])
                        last.then_inc(s["hT_ps"], 1)
                    j = t - 1
                    if j >= 0:
                        n = i * BLOCKS + j
                        pe.wait_ge(s["eT"], done(n))
                        pe.wait_ge(s["sum"], freed(n, 2))
                        for k in range(4):
                            w = (wn if k < 2 else wo)[:, k % 2, :]
                            last = nc.tensor.matmul(pb[2 + j % 2][:, 0:F], hsT[:, j % 2, k * P:(k + 1) * P], w,
                                                    start=(k == 0), stop=(k == 3))
                        last.then_inc(s["mm"], 1)

        @block.vector
        def _(dve):
            V = nc.vector
            for s in node_sems:
                give_credit(dve, [s[k] for k in NODE_DVE if k in s])
            for s in edge_sems:
                give_credit(dve, [s[k] for k in EDGE_DVE if k in s])
            for s in sorts:
                give_credit(dve, [s["hot"], s["pos"]])

            def sort(which, s):
                count = [0]

                def link(ins):
                    count[0] += 1
                    ins.then_inc(s["link"], 1)
                    dve.wait_ge(s["link"], count[0])

                width = 2 + which
                full, rest = E // C, E % C
                fold = full // 16 * 16
                if which == 1:
                    dve.wait_ge(sorts[0]["loaded"], 16)
                    dve.wait_ge(sorts[0]["rec"], done(C // COLS - 1))
                link(V.memset(key_int[96:P, :], NB * P))
                link(V.memset(oth_int[96:P, :], 0))
                if which == 1:
                    link(V.memset(key_blk[96:P, :], 0.0))
                dve.sem_inc(s["keys"], 1)
                n_in = (fold > 0) + (full > fold) + (rest > 0)
                dve.wait_ge(s["in"], 16 * n_in * width)
                if which == 1:
                    link(V.tensor_copy(rec_all[:, :, 2], key_blk[:, :]))
                else:
                    link(V.memset(rec_all[:, :, 2], 0.0))
                link(V.tensor_scalar(blk_int[:, :], key_int[:, :], 7, None, ALU.arith_shift_right))
                link(V.tensor_copy(key_blk[:, :], blk_int[:, :]))
                link(V.tensor_copy(rec_all[:, :, 0], key_int[:, :]))
                link(V.scalar_tensor_tensor(rec_all[:, :, 0], key_blk[:, :], -float(P), rec_all[:, :, 0],
                                            ALU.mult, ALU.add))
                link(V.tensor_scalar(rec_all[:, :, 1], oth_int[:, :], 0, N - 1, ALU.max, ALU.min))
                ev = empty[:, 0:NT * width].rearrange("p (t w) -> p t w", w=width)
                link(V.memset(ev[:, :, 0], -1.0))
                link(V.memset(ev[:, :, 1:width], 0.0))
                dve.sem_inc(s["empty_ms"], 1)
                dve.wait_ge(s_const, 9)
                steps = C // COUNT_COLS
                with dve.Fori(0, steps // 2) as i:
                    for par in range(2):
                        n = i * 2 + par
                        dve.wait_ge(s["add"], freed(n, 2))
                        V.tensor_tensor(hot_cnt[:, par, :, :],
                                        iota_n[:, 0:KB].unsqueeze(1).to_broadcast([P, COUNT_COLS, KB]),
                                        key_blk[:, bass.ds(n * COUNT_COLS, COUNT_COLS)].unsqueeze(2).to_broadcast(
                                            [P, COUNT_COLS, KB]), ALU.is_equal).then_inc(s["hot"], 1)
                dve.wait_ge(s["add"], done(steps - 1))
                link(V.tensor_reduce(cnt[:, :], pb[0][:, 0:COUNT_COLS * KB].rearrange("p (c b) -> p b c", b=KB),
                                     AX.X, ALU.add))
                dve.sem_inc(s["cnt"], 1)
                dve.wait_ge(s["sums"], 1)
                link(V.tensor_scalar(tot[:, :], pb[2][:, 0:KB], float(P - 1), None, ALU.add))
                link(V.tensor_copy(tot_i[:, :], tot[:, :]))
                link(V.tensor_scalar(tot_i[:, :], tot_i[:, :], 7, None, ALU.arith_shift_right))
                link(V.tensor_copy(ntile[:, :], tot_i[:, :]))
                link(V.tensor_tensor_scan(tend[:, :], ones[:, 0:KB], ntile[:, :], 0.0, ALU.mult, ALU.add))
                link(V.tensor_tensor(nxt[:, :], tend[:, :], ntile[:, :], ALU.subtract))
                link(V.scalar_tensor_tensor(nxt[:, :], nxt[:, :], float(P), pb[1][:, 0:KB], ALU.mult, ALU.add))
                for j in range(GRID):
                    link(V.tensor_scalar(junk[:, :], tend[:, :], grid[:, j:j + 1], 0.0, ALU.is_le, ALU.add,
                                         accum_out=blk_f[:, j:j + 1]))
                link(V.tensor_scalar(blk_i[:, :], blk_f[:, :], float(NB), None, ALU.min))
                dve.sem_inc(s["brow"], 1)
                dve.sem_inc(s["base"], 1)
                dve.sem_inc(s["chain"], 1)

                def positions(i):
                    for par in range(2):
                        n = i * 2 + par
                        for u in range(COLS):
                            kb = key_blk[:, bass.ds(n * COLS + u, 1)]
                            dve.wait_ge(s["chain"], n * COLS + u + 1)
                            V.scalar_tensor_tensor(junk[:, :], iota_n[:, 0:KB], kb, nxt[:, :], ALU.is_equal,
                                                   ALU.mult, accum_out=slot_f[:, u:u + 1])
                            V.scalar_tensor_tensor(nxt[:, :], iota_n[:, 0:KB], kb, nxt[:, :], ALU.is_equal,
                                                   ALU.add).then_inc(s["chain"], 1)
                        dve.wait_ge(s["chain"], n * COLS + COLS + 1)
                        V.tensor_copy(slot_i[:, :], slot_f[:, :]).then_inc(s["conv"], 1)
                        dve.wait_ge(s["conv"], n * 3 + 1)
                        V.tensor_scalar(lane_i[:, :], slot_i[:, :], P - 1, None, ALU.bitwise_and)
                        V.tensor_scalar(tile_i[:, :], slot_i[:, :], 7, None, ALU.arith_shift_right).then_inc(s["conv"], 1)
                        dve.wait_ge(s["conv"], n * 3 + 2)
                        V.tensor_copy(lane_f[:, :], lane_i[:, :])
                        V.tensor_copy(tile_f[:, :], tile_i[:, :]).then_inc(s["conv"], 1)
                        dve.wait_ge(s["conv"], n * 3 + 3)
                        if not isinstance(i, int):
                            dve.wait_ge(s[f"out{par}"], i * (16 * COLS))
                        V.scalar_tensor_tensor(pos_ring[:, par, :], lane_f[:, :], float(NT), tile_f[:, :], ALU.mult,
                                               ALU.add).then_inc(s["pos"], 1)
                positions(0)
                with dve.Fori(1, C // COLS // 2) as i:
                    positions(i)

            for which, s in enumerate(sorts):
                sort(which, s)

            def normalise(src14, eps, s, k, turn, i, lanes=1):
                base = turn * 4
                for j in range(BLOCKS):
                    last = V.bn_stats(st6[:, j, :], src14[:, j, :])
                last.then_inc(s["part"], 1)
                dve.wait_ge(s["part"], base + 1)
                dve.sem_inc(s_past, 1)
                for j in range(BLOCKS):
                    last = V.bn_aggr(mv[:, j, :], st6[:, j, :])
                last.then_inc(s["part"], 1)
                dve.wait_ge(s["part"], base + 2)
                V.tensor_scalar(sd[:, :], mv[:, :, 1], eps, None, ALU.add).then_inc(s["st"], 1)
                dve.wait_ge(s["sqrt"], turn + 1)
                V.reciprocal(rs[:, :], sd[:, :]).then_inc(s["part"], 1)
                dve.wait_ge(s["part"], base + 3)
                V.scalar_tensor_tensor(nb[:, :], mv[:, :, 0], -1.0, rs[:, :], ALU.mult, ALU.mult).then_inc(s["part"], 1)
                dve.wait_ge(s["part"], base + 4)

            s = node_sems[0]
            dve.wait_ge(s_w, 16 * 18)
            V.tensor_tensor(pbias[:, 0, :], pbias[:, 0, :], pbias[:, 1, :], ALU.add).then_inc(s["link"], 1)
            dve.wait_ge(s["link"], 1)
            with dve.Fori(0, NODE_STEPS) as i:
                dve.wait_ge(s["x"], i * 32 + 32)
                normalise(x14, EPS, s, 0, i, i)
                dve.sem_inc(s["rs"], 1)
                for t in range(BLOCKS + 4):
                    j = t
                    if j < BLOCKS:
                        n = i * BLOCKS + j
                        dve.wait_ge(s["hT_ps"], done(n))
                        dve.wait_ge(s["mm"], freed(n, 2))
                        V.tensor_copy(hsT[:, j % 2, 0:2 * P], pb[j % 2][:, 0:2 * P]).then_inc(s["hT"], 1)
                    j = t - 1
                    if 0 <= j < BLOCKS:
                        n = i * BLOCKS + j
                        dve.wait_ge(s["mm"], done(n))
                        V.tensor_tensor(e14[:, j, :], pb[2 + j % 2][:, 0:D], pbias[:, 0, :], ALU.add).then_inc(s["emb"], 1)
                    j = t - 4
                    if 0 <= j < BLOCKS:
                        n = i * BLOCKS + j
                        dve.wait_ge(s["kv"], done(n))
                        V.tensor_copy(q_sb[:, bass.ds(n, 1), :], pw[1][:, j % 2, 0:D].unsqueeze(1)).then_inc(s["q"], 1)

            def add_tile(s, n, u, buf, blk, to, width):
                if u == 0:
                    dve.wait_ge(s["agg"], done(n))
                dve.wait_ge(s["add"], n * TILES + (u + CREDIT))
                last = V.tensor_tensor(to[:, bass.ds(blk, 1), :], to[:, bass.ds(blk, 1), :],
                                       pw4(buf)[:, u:u + 1, 0:width], ALU.add)
                last.then_inc(s["add"], 1)

            def attention(which):
                s = edge_sems[which]
                dve.wait_ge(node_sems[which]["out"], 32 * NODE_STEPS)
                dve.wait_ge(s["clear"], 1)
                with dve.Fori(0, EDGE_STEPS) as i:
                    for t in range(GROUPS + 4):
                        a, b, c = t, t - 2, t - 4
                        hots, scores, sums = a < GROUPS, 0 <= b < GROUPS, c >= 0
                        na, n, nc_ = i * GROUPS + a, i * GROUPS + b, i * GROUPS + c
                        if sums:
                            blks = tile_blocks(mybir.EngineType.DVE, nc_)
                        r = b % RING
                        if scores:
                            dve.wait_ge(s["q"], done(n))
                            dve.wait_ge(s_rows[r], rows_in(which, i, b))
                            V.tensor_tensor(prod.rearrange("p (t d) -> p t d", t=TILES),
                                            pb[2 + b % 2][:, :].rearrange("p (t d) -> p t d", t=TILES),
                                            rows[:, r, :, 0:D], ALU.mult).then_inc(s["prod"], 1)
                        if sums:
                            add_tile(s, nc_, 0, c % 2, blks[0], agg_sb, MSG)
                        if scores:
                            dve.wait_ge(s["prod"], done(n))
                            V.tensor_reduce(score[:, b % 2, :], prod.rearrange("p (h d) -> p h d", d=HD),
                                            AX.X, ALU.add).then_inc(s["score"], 1)
                        if sums:
                            add_tile(s, nc_, 1, c % 2, blks[1], agg_sb, MSG)
                        if scores:
                            dve.wait_ge(s["score"], done(n))
                            V.tensor_scalar(score[:, b % 2, :], score[:, b % 2, :], 10.0, -10.0, ALU.min, ALU.max)\
                                .then_inc(s["clip"], 1)
                        if hots:
                            for u in range(TILES):
                                last = V.tensor_scalar(hot16[:, a % 2, u, :], iota16[:, :],
                                                       slot_src[:, bass.ds(na * TILES + u, 1), 0], None,
                                                       ALU.is_equal)
                            last.then_inc(s["hot"], 1)
                        if sums:
                            add_tile(s, nc_, 2, c % 2, blks[2], agg_sb, MSG)
                            add_tile(s, nc_, 3, c % 2, blks[3], agg_sb, MSG)
                        if scores:
                            dve.wait_ge(s["exp"], done(n))
                            V.tensor_tensor(msg[:, b % 2, :, 0:D].rearrange("p t (h d) -> p t h d", d=HD),
                                            rows[:, r, :, D:2 * D].rearrange("p t (h d) -> p t h d", d=HD),
                                            msg[:, b % 2, :, D:MSG].unsqueeze(3).to_broadcast([P, TILES, H, HD]),
                                            ALU.mult).then_inc(s["msg"], 1)

            def layer_out(s, layer, i):
                count = [0]
                LINKS = 7

                def link(ins):
                    count[0] += 1
                    ins.then_inc(s["link"], 1)
                    dve.wait_ge(s["link"], i * LINKS + count[0])

                step = bass.ds(i * BLOCKS, BLOCKS)
                heads = [P, BLOCKS, H, HD]
                link(V.tensor_scalar(rnorm[:, :, :], agg_sb[:, step, D:MSG], 1e-8, None, ALU.add))
                link(V.reciprocal(rnorm[:, :, :], rnorm[:, :, :]))
                link(V.tensor_tensor(y14[:, :, :].rearrange("p b (h d) -> p b h d", d=HD),
                                     agg_sb[:, step, 0:D].rearrange("p b (h d) -> p b h d", d=HD),
                                     rnorm[:, :, :].unsqueeze(3).to_broadcast(heads), ALU.mult))
                dve.sem_inc(s["used"], 1)
                link(V.tensor_tensor(y14[:, :, :], y14[:, :, :], e14[:, :, :], ALU.add))
                normalise(y14, 1e-6, s, 0, i * (1 + layer), i)
                for j in range(BLOCKS):
                    last = V.tensor_scalar(y14[:, j, :], y14[:, j, :], rs[:, j:j + 1], nb[:, j:j + 1], ALU.mult, ALU.add)
                link(last)
                rowb = [P, BLOCKS, D]
                link(V.tensor_tensor(e14[:, :, :], y14[:, :, :], lns[:, layer, 0, :].unsqueeze(1).to_broadcast(rowb),
                                     ALU.mult))
                link(V.tensor_tensor(e14[:, :, :], e14[:, :, :], lns[:, layer, 1, :].unsqueeze(1).to_broadcast(rowb),
                                     ALU.add))
                assert count[0] == LINKS
                dve.sem_inc(s["y"], 1)

            dve.wait_ge(sorts[0]["row"], 32)
            attention(0)
            s = node_sems[1]
            with dve.Fori(0, NODE_STEPS) as i:
                dve.wait_ge(s["e"], i * 16 + 16)
                layer_out(s, 0, i)
                for j in range(BLOCKS):
                    n = i * BLOCKS + j
                    dve.wait_ge(s["kv"], done(n))
                    V.tensor_copy(q_sb[:, bass.ds(n, 1), :], pw[1][:, j % 2, 0:D].unsqueeze(1)).then_inc(s["q"], 1)
            attention(1)
            s = node_sems[2]
            with dve.Fori(0, NODE_STEPS) as i:
                dve.wait_ge(s["e"], i * 16 + 16)
                dve.wait_ge(s["x"], i * 32 + 32)
                layer_out(s, 1, i)
                for j in range(BLOCKS):
                    n = i * BLOCKS + j
                    dve.wait_ge(s["qkv"], done(n))
                    V.tensor_tensor(o14[:, j, :], pw[1][:, j % 2, 0:F], invb[:, :], ALU.add).then_inc(s["q"], 1)
                    dve.wait_ge(s["q"], done(n))
                    V.tensor_tensor(o14[:, j, :], o14[:, j, :], x14[:, j, :], ALU.add).then_inc(s["sum"], 1)
                dve.wait_ge(s["sum"], done(i * BLOCKS + BLOCKS - 1))
                normalise(o14, EPS, s, 0, i * 2 + 1, i)
                dve.sem_inc(s["rs"], 1)
            s = edge_sems[2]
            dve.wait_ge(sorts[1]["row"], 32)
            dve.wait_ge(node_sems[2]["out"], 32 * NODE_STEPS)
            dve.wait_ge(s["clear"], 1)
            with dve.Fori(0, EDGE_STEPS) as i:
                for t in range(GROUPS + 2):
                    a, c = t, t - 2
                    na, nc_ = i * GROUPS + a, i * GROUPS + c
                    if c >= 0:
                        blks = tile_blocks(mybir.EngineType.DVE, nc_)
                    for u in range(TILES):
                        if c >= 0:
                            add_tile(s, nc_, u, c % 2, blks[u], conv_sb, F)
                        if a < GROUPS:
                            at = bass.ds(na * TILES + u, 1)
                            last = V.tensor_scalar(hot[:, a % HOTS, u, :], iota_n[:, :], slot_dst[:, at, 0],
                                                   slot_dst[:, at, 2], ALU.is_equal, ALU.mult)
                            if u == TILES - 1:
                                last.then_inc(s["hot"], 1)
            s = node_sems[3]
            with dve.Fori(0, NODE_STEPS) as i:
                dve.wait_ge(s["e"], i * 16 + 16)
                for j in range(BLOCKS):
                    n = i * BLOCKS + j
                    dve.wait_ge(s["mm"], done(n))
                    V.tensor_tensor(o14[:, j, :], pb[2 + j % 2][:, 0:F], o14[:, j, :], ALU.add).then_inc(s["q"], 1)
                    dve.wait_ge(s["q"], done(n))
                    V.tensor_tensor(o14[:, j, :], o14[:, j, :], cbias[:, :], ALU.add).then_inc(s["sum"], 1)


_INS = ['x', 'src', 'dst', 'edge_weight', 'L0_gnn_W_P_w', 'L0_gnn_W_P_b', 'L0_gnn_W_pos', 'L0_gnn_q1', 'L0_gnn_k1',
        'L0_gnn_v1', 'L0_gnn_ln1_s', 'L0_gnn_ln1_b', 'L0_gnn_q2', 'L0_gnn_k2', 'L0_gnn_v2', 'L0_gnn_ln2_s',
        'L0_gnn_ln2_b', 'L0_gnn_inv_w', 'L0_gnn_inv_b', 'L1_gnn_w_nbr', 'L1_gnn_w_own', 'L1_gnn_bias']


def kernel(**inputs):
    import numpy as _np
    import concourse.bacc as _bacc
    from concourse import mybir as _mybir
    from concourse.bass_utils import run_bass_kernel_spmd as _run

    nc = _bacc.Bacc("TRN2", target_bir_lowering=False, num_devices=1)
    arrays, args = {}, []
    for name in _INS:
        a = _np.ascontiguousarray(inputs[name])
        arrays[f"in_{name}_dram"] = a
        args.append(nc.dram_tensor(f"in_{name}_dram", a.shape, _mybir.dt.from_np(a.dtype), kind="ExternalInput").ap())
    shape = tuple(inputs["x"].shape)
    args.append(nc.dram_tensor("out_0_dram", shape, _mybir.dt.float32, kind="ExternalOutput").ap())
    gnn_kernel(nc, *args)
    r = _run(nc, [arrays], core_ids=[0])
    return r.results[0]["out_0_dram"]
```

```python
import concourse.bass as bass
from concourse import mybir
from contextlib import ExitStack

P = 128
FP32 = mybir.dt.float32
BF16 = mybir.dt.bfloat16
I32 = mybir.dt.int32
U32 = mybir.dt.uint32
I16 = mybir.dt.int16
ALU = mybir.AluOpType
ACT = mybir.ActivationFunctionType
AX = mybir.AxisListType

BLOCKS = 14
TILES = 4
GROUPS = 20
RING = 5
HOTS = 4
CREDIT = 5
COLS = 8


def cdiv(a, b):
    return -(-a // b)


def done(n):
    return n + (1 + CREDIT)


def freed(n, slots):
    return n + (1 + CREDIT - slots)


def gnn_kernel(nc, x, src, dst, edge_weight, W_P_w, W_P_b, W_pos, q1, k1, v1, ln1_s, ln1_b,
               q2, k2, v2, ln2_s, ln2_b, inv_w, inv_b, w_nbr, w_own, bias, out):
    N, F = x.shape
    E = src.shape[0]
    D = q1.shape[0]
    H = 8
    HD = D // H
    MSG = D + H
    NB = cdiv(N, P)
    LAST = N - (NB - 1) * P
    KB = NB + 1
    KC = cdiv(KB, 2) * 2
    C = cdiv(cdiv(E + P, P), 2 * COLS) * 2 * COLS
    STEPS = C // COLS // 2
    NT = cdiv(cdiv(C * P + KB * (P - 1), P), TILES * GROUPS) * TILES * GROUPS
    GRID = cdiv(NT, P)
    NODE_STEPS = NB // BLOCKS
    EDGE_STEPS = NT // (TILES * GROUPS)
    EPS = 1e-5
    CHUNK = P * 3
    assert NB % BLOCKS == 0 and D == P and F == 2 * P and STEPS <= KB

    ctx = ExitStack()
    with ctx:
        def sb(name, shape, dt=FP32):
            return ctx.enter_context(nc.sbuf_tensor(name, shape, dt))

        def sem(name):
            return ctx.enter_context(nc.semaphore(name))

        def dram(name, shape, dt=FP32):
            return nc.dram_tensor(name, shape, dt, kind="Internal").ap()

        kv_table = dram("kv_table", (NB * P, 2 * D))
        kv_table2 = dram("kv_table2", (NB * P, 2 * D))
        emb1_dram = dram("emb1_dram", (NB * P, D))
        emb2_dram = dram("emb2_dram", (NB * P, D))
        x1_dram = dram("x1_dram", (NB * P, F))
        h_table = dram("h_table", (NB * P, F))
        edge_rec = dram("edge_rec", (C, CHUNK))
        slots_src = dram("slots_src", (P * NT, 2))
        slots_dst = dram("slots_dst", (P * NT, 3))
        blocks_src = dram("blocks_src", (P * GRID,), I16)
        blocks_dst = dram("blocks_dst", (P * GRID,), I16)

        node_mem = sb("node_mem", [P, KB * max(MSG + D, F)])
        q_sb = node_mem[:, 0:KB * D].rearrange("p (b d) -> p b d", d=D)
        agg_sb = node_mem[:, KB * D:KB * (D + MSG)].rearrange("p (b d) -> p b d", d=MSG)
        conv_sb = node_mem[:, 0:KB * F].rearrange("p (b d) -> p b d", d=F)
        s0 = KB * D
        key_int = node_mem[:, 0:C].bitcast(I32)
        oth_int = node_mem[:, C:2 * C].bitcast(I32)
        wgt = node_mem[:, 2 * C:3 * C]
        edges = node_mem[:, 3 * C:6 * C].rearrange("p (c w) -> p c w", w=3)
        blk_int = node_mem[:, 6 * C:7 * C].bitcast(I32)
        key16 = node_mem[:, 7 * C:7 * C + C // 2].bitcast(BF16)
        assert 8 * C <= KB * D
        key_blk = node_mem[:, s0:s0 + C]
        rec_src = node_mem[:, s0 + C:s0 + 3 * C].rearrange("p (c w) -> p c w", w=2)
        dst16 = node_mem[:, s0 + 4 * C:s0 + 4 * C + C // 2].bitcast(BF16)
        descents = node_mem[:, s0 + 4 * C:s0 + 5 * C]
        junk16 = node_mem[:, s0 + 5 * C:s0 + 6 * C].bitcast(BF16).rearrange("p (a c) -> p a c", a=2)
        G3 = GRID * CHUNK
        by_tile = node_mem[:, s0:s0 + G3].rearrange("p (j e w) -> p j e w", j=GRID, w=3)
        by_lane = node_mem[:, s0 + G3:s0 + 2 * G3].rearrange("p (t j w) -> p j t w", j=GRID, w=3)
        by_lane_flat = node_mem[:, s0 + G3:s0 + 2 * G3]
        rec_dst = node_mem[:, s0 + C:s0 + 4 * C].rearrange("p (c w) -> p c w", w=3)
        dblk_int = node_mem[:, s0 + 4 * C:s0 + 5 * C].bitcast(I32)
        empty_dst = node_mem[:, s0 + 5 * C:s0 + 5 * C + 3 * NT].rearrange("p (t w) -> p t w", w=3)
        assert 6 * C <= KB * MSG and 5 * C + 3 * NT <= KB * MSG and 2 * G3 <= KB * MSG

        slot_mem = sb("slot_mem", [P, NT * 3])
        slot_src = slot_mem[:, 0:NT * 2].rearrange("p (t w) -> p t w", w=2)
        slot_dst = slot_mem[:, :].rearrange("p (t w) -> p t w", w=3)
        empty_src = slot_src
        gidx = sb("gidx", [P, NT], U32)
        blk_row = sb("blk_row", [1, P * GRID], I16)
        idx_ring = sb("idx_ring", [P, RING, TILES], U32)

        RINGW = RING * TILES * F
        GW = TILES * P
        work = sb("work", [P, BLOCKS * 3 * F])
        rows = work[:, 0:RINGW].rearrange("p (g t f) -> p g t f", g=RING, t=TILES)
        o = RINGW
        hot = work[:, o:o + HOTS * GW].rearrange("p (g t n) -> p g t n", g=HOTS, t=TILES)
        o += HOTS * GW
        hotT = work[:, o:o + 2 * GW].rearrange("p (g n) -> p g n", g=2)
        o += 2 * GW
        hot16 = work[:, o:o + GW].bitcast(BF16).rearrange("p (g t n) -> p g t n", g=2, t=TILES)
        o += GW
        prod = work[:, o:o + GW]
        o += GW
        msg = work[:, o:o + 2 * TILES * MSG].rearrange("p (g t m) -> p g t m", g=2, t=TILES)
        assert o + 2 * TILES * MSG <= BLOCKS * 3 * F
        x14 = work[:, 0:BLOCKS * F].rearrange("p (b f) -> p b f", f=F)
        o14 = work[:, BLOCKS * F:2 * BLOCKS * F].rearrange("p (b f) -> p b f", f=F)
        e14 = work[:, 2 * BLOCKS * F:BLOCKS * (2 * F + D)].rearrange("p (b f) -> p b f", f=D)
        c14 = work[:, 2 * BLOCKS * F:3 * BLOCKS * F].rearrange("p (b f) -> p b f", f=F)
        y14 = work[:, BLOCKS * (2 * F + D):BLOCKS * (2 * F + 2 * D)].rearrange("p (b f) -> p b f", f=D)

        hs = sb("hs", [P, 2, F])
        hsT = sb("hsT", [P, 2, 2 * F])
        eT = sb("eT", [P, 2, D])
        score = sb("score", [P, 2, TILES * H])

        wp = sb("wp", [P, 2, D])
        wqkv1 = sb("wqkv1", [P, 3 * D])
        wqkv2 = sb("wqkv2", [P, 3 * D])
        winv = sb("winv", [P, F])
        wn = sb("wn", [P, 2, F])
        wo = sb("wo", [P, 2, F])
        pbias = sb("pbias", [P, 2, D])
        lns = sb("lns", [P, 2, 2, D])
        invb = sb("invb", [P, F])
        cbias = sb("cbias", [P, F])

        st6 = sb("st6", [P, BLOCKS, 6])
        mv = sb("mv", [P, BLOCKS, 2])
        sd = sb("sd", [P, BLOCKS])
        rs = sb("rs", [P, BLOCKS])
        nb = sb("nb", [P, BLOCKS])
        rnorm = sb("rnorm", [P, BLOCKS, H])

        iota_n = sb("iota_n", [P, P])
        iota16 = sb("iota16", [P, P], BF16)
        ident = sb("ident", [P, P])
        ident16 = sb("ident16", [P, P], BF16)
        below = sb("below", [P, P])
        ones = sb("ones", [P, P])
        grid = sb("grid", [P, GRID])
        cnt_src = sb("cnt_src", [P, KC])
        cnt_dst = sb("cnt_dst", [P, KC])
        next_int = sb("next_int", [P, 1], I32)
        next_f = sb("next_f", [P, 1])
        viol = sb("viol", [P, 2])
        flag_f = sb("flag_f", [P, 1])
        flag = sb("flag", [P, 1], I32)
        end = sb("end", [P, KB])
        c_end = sb("c_end", [P, KB])
        c_start = sb("c_start", [P, KB])
        c_stop = sb("c_stop", [P, KB])
        shift = sb("shift", [P, KB])
        chunk_f = sb("chunk_f", [P, GRID])
        chunk = sb("chunk", [P, GRID], U32)
        node0 = sb("node0", [P, GRID])
        tot = sb("tot", [P, KB])
        tot_i = sb("tot_i", [P, KB], I32)
        ntile = sb("ntile", [P, KB])
        tend = sb("tend", [P, KB])
        nxt = sb("nxt", [P, KB])
        junk = sb("junk", [P, KB])
        blk_f = sb("blk_f", [P, GRID])
        blk_i = sb("blk_i", [P, GRID], I16)
        slot_f = sb("slot_f", [P, COLS])
        slot_i = sb("slot_i", [P, COLS], I32)
        lane_i = sb("lane_i", [P, COLS], I32)
        tile_i = sb("tile_i", [P, COLS], I32)
        tile_f = sb("tile_f", [P, COLS])
        lane_f = sb("lane_f", [P, COLS])
        pos_ring = sb("pos_ring", [P, 2, COLS], U32)
        rec_ring = sb("rec_ring", [P, 2, COLS, 3])

        pb = [ctx.enter_context(nc.psum_tensor(f"pb{n}", [P, 512], FP32)) for n in range(4)]
        pw = [ctx.enter_context(nc.psum_tensor(f"pw{n}", [P, 2, 512], FP32)) for n in range(2)]

        hotT_ps = [pb[n][:, 0:GW // 2].bitcast(BF16) for n in range(2)]

        def pw4(n):
            return pw[n][:, :, :].rearrange("p a (b c) -> p (a b) c", b=2)

        s_const = sem("s_const")
        s_id16 = sem("s_id16")
        s_past = sem("s_past")
        s_w = sem("s_w")
        IN = 16 * (3 * ((E // C >= 16) + (E // C % 16 > 0) + (E % C > 0)) + 1 + (E % C > 0))
        s_big = [sem(f"s_big{k}") for k in range(2)]

        def names(tag, *what):
            return {w: sem(f"{tag}_{w}") for w in what}

        SCATTER = ("link", "empty_ms", "empty", "brow", "row", "base", "chain", "conv", "pos", "rec", "out0", "out1")
        src_sort = names("src_sort", "keys", "in", "edges", "cnt", "sums", "loaded", "gidx", *SCATTER)
        dst_sort = names("dst_sort", "in", "sums", *SCATTER)
        order = names("order", "edges", "link", "cnt", "sums", "brow", "row", "chunk", "rows", "node0",
                      "turned", "lanes", "slots", "loaded", "gidx")
        s_flag = sem("s_flag")
        sorts = [src_sort, order]
        node_sems = [
            names("n0", "x", "link", "st", "sqrt", "rs", "h", "hT_ps", "hT", "mm", "emb", "eT_ps", "eT", "qkv",
                  "q", "kv", "part", "out"),
            names("n1", "e", "link", "st", "sqrt", "eT_ps", "eT", "qkv", "q", "kv", "y", "used", "part", "out"),
            names("n2", "x", "e", "link", "st", "sqrt", "rs", "h", "eT_ps", "eT", "qkv", "q", "y", "used", "sum",
                  "part", "out"),
            names("n3", "c", "x", "e", "hT_ps", "eT", "q", "mm", "sum", "out")]
        s_idx = [sem(f"s_idx{r}") for r in range(RING)]
        s_rows = [sem(f"s_rows{r}") for r in range(RING)]

        def idx_in(which, i, g):
            return 16 * (i * (GROUPS // RING) + (g // RING + 1 + which * EDGE_STEPS * (GROUPS // RING)))

        def rows_in(which, i, g):
            return 16 * TILES * (i * (GROUPS // RING) + (g // RING + 1 + which * EDGE_STEPS * (GROUPS // RING)))

        edge_sems = [names(t, "hot", "hotT_ps", "hotT", "q", "prod", "score", "clip", "exp", "msg", "agg",
                           "add", "clear", "hot32") for t in ("e0", "e1")]
        edge_sems.append(names("e2", "hot", "agg", "add", "clear"))

        block = ctx.enter_context(nc.Block())

        def tile_blocks(engine, n):
            _, values = nc.values_load_multi_w_load_instructions(
                blk_row[0:1, bass.ds(n * TILES, TILES)], engines=[engine], min_val=0, max_val=KB - 1,
                skip_runtime_bounds_check_because="the sort caps each at the last block")
            return values

        def unordered(engine):
            _, values = nc.values_load_multi_w_load_instructions(
                flag[0:1, 0:1], engines=[engine], min_val=0, max_val=1,
                skip_runtime_bounds_check_because="it is a minimum with 1")
            return values[0]

        def give_credit(eng, sems):
            for s in sems:
                eng.sem_inc(s, CREDIT)

        NODE_DVE = ("hT", "emb", "q", "sum")
        NODE_ACT = ("h", "eT", "kv")
        NODE_PE = ("hT_ps", "mm", "eT_ps", "qkv")
        EDGE_DVE = ("hot", "prod", "score", "clip", "msg", "add")
        EDGE_ACT = ("hot32", "hotT", "exp")
        EDGE_PE = ("hotT_ps", "q", "agg")

        @block.sync
        def _(sp):
            def row(v):
                return v.rearrange("(a n) -> a n", a=1) if len(v.shape) == 1 else v

            for ap, s in ((wp[:, :, :], W_P_w.rearrange("(k p) n -> p k n", p=P)),
                          (wn[:, :, :], w_nbr.rearrange("(k p) n -> p k n", p=P)),
                          (wo[:, :, :], w_own.rearrange("(k p) n -> p k n", p=P)),
                          (winv[:, :], inv_w),
                          (wqkv1[:, 0:D], q1), (wqkv1[:, D:2 * D], k1), (wqkv1[:, 2 * D:3 * D], v1),
                          (wqkv2[:, 0:D], q2), (wqkv2[:, D:2 * D], k2), (wqkv2[:, 2 * D:3 * D], v2)):
                sp.dma_start(ap, s).then_inc(s_w, 16)
            for ap, s in ((pbias[:, 0, :], W_P_b), (pbias[:, 1, :], W_pos),
                          (lns[:, 0, 0, :], ln1_s), (lns[:, 0, 1, :], ln1_b),
                          (lns[:, 1, 0, :], ln2_s), (lns[:, 1, 1, :], ln2_b),
                          (invb[:, :], inv_b), (cbias[:, :], bias)):
                w = row(s)
                sp.dma_start(ap, w.to_broadcast([P, w.shape[1]])).then_inc(s_w, 16)

            def load_lists(which):
                s = sorts[which]
                slots, to = ((slots_src, slot_src), (slots_dst, slot_dst))[which]
                sp.dma_start(to[:, :, :], slots.rearrange("(p t) w -> p t w", p=P)).then_inc(s["loaded"], 16)
                sp.dma_start(blk_row[:, :], (blocks_src, blocks_dst)[which].rearrange("(a n) -> a n", a=1))\
                    .then_inc(s["row"], 16)

            def store_blocks(s, to):
                sp.wait_ge(s["brow"], 1)
                sp.dma_start(to.rearrange("(p c) -> p c", p=P), blk_i[:, :]).then_inc(s["row"], 16)
                sp.wait_ge(s["row"], 16)

            def scattered(s):
                for par in range(2):
                    sp.wait_ge(s[f"out{par}"], 16 * COLS * STEPS)

            s = src_sort
            full, rest = E // C, E % C
            fold = full // 16 * 16
            sp.wait_ge(s["keys"], 1)
            for v, to in ((src, key_int), (dst, oth_int), (edge_weight, wgt)):
                for a, b in ((0, fold), (fold, full)):
                    if b > a:
                        sp.dma_start(to[a:b, :], v[a * C:b * C].rearrange("(p c) -> p c", c=C)).then_inc(s["in"], 16)
                if rest:
                    sp.dma_start(to[full:full + 1, 0:rest],
                                 v[full * C:E].rearrange("(p c) -> p c", p=1)).then_inc(s["in"], 16)
            with nc.allow_non_contiguous_dma(reason="one element of a partition, once"):
                sp.dma_start(next_int[0:full - 1, :], dst[C:full * C].rearrange("(p c) -> p c", c=C)[:, 0:1])\
                    .then_inc(s["in"], 16)
            if rest:
                sp.dma_start(next_int[full - 1:full, :],
                             dst[full * C:full * C + 1].rearrange("(p c) -> p c", p=1)).then_inc(s["in"], 16)
            sp.wait_ge(s["empty_ms"], 1)
            sp.dma_start(slots_src.rearrange("(p t) w -> p t w", p=P), empty_src[:, :, :]).then_inc(s["empty"], 16)
            sp.wait_ge(s["edges"], 2)
            sp.dma_start(edge_rec.rearrange("a b -> (a b)").rearrange("(p c w) -> p c w", p=P, w=3), edges[:, :, :])\
                .then_inc(order["edges"], 16)
            store_blocks(s, blocks_src)
            scattered(s)
            load_lists(0)

            store_blocks(order, blocks_dst)
            sp.wait_ge(order["lanes"], GRID)
            sp.dma_start(slots_dst.rearrange("(p t) w -> p (t w)", p=P), by_lane_flat[:, 0:NT * 3]).then_inc(order["slots"], 16)
            sp.wait_ge(order["slots"], 16)
            sp.wait_ge(s_flag, 1)
            with sp.If(unordered(mybir.EngineType.SP)):
                s = dst_sort
                sp.dma_start(rec_dst[:, :, :], edge_rec.rearrange("a b -> (a b)").rearrange("(p c w) -> p c w", p=P, w=3))\
                    .then_inc(s["in"], 16)
                sp.wait_ge(s["empty_ms"], 1)
                sp.dma_start(slots_dst.rearrange("(p t) w -> p t w", p=P), empty_dst[:, :, :]).then_inc(s["empty"], 16)
                store_blocks(s, blocks_dst)
                scattered(s)

            def rows_of(table, i):
                return table[bass.ds(i * (BLOCKS * P), BLOCKS * P), :].rearrange("(b p) f -> p b f", p=P)

            def ragged(i, last):
                whole = BLOCKS - 1
                n = LAST if last else P
                return (whole, slice(0, P), bass.ds(i * (BLOCKS * P), whole * P)), \
                       (whole, slice(0, n), bass.ds(i * (BLOCKS * P) + whole * P, n))

            def load_x(i, last, s_in):
                (w, _, a), (_, lanes, b) = ragged(i, last)
                sp.dma_start(x14[:, 0:w, :], x[a, :].rearrange("(b p) f -> p b f", p=P)).then_inc(s_in, 16)
                sp.dma_start(x14[lanes, w, :], x[b, :]).then_inc(s_in, 16)

            def node_loop(step):
                if NODE_STEPS > 1:
                    with sp.Fori(0, NODE_STEPS - 1) as i:
                        step(i, False)
                step(NODE_STEPS - 1, True)

            sp.wait_ge(s_const, 9)

            def stage0(i, last):
                s = node_sems[0]
                load_x(i, last, s["x"])
                sp.wait_ge(s["emb"], done(i * BLOCKS + BLOCKS - 1))
                sp.dma_start(rows_of(emb1_dram, i), e14[:, :, :]).then_inc(s["out"], 16)
                sp.wait_ge(s["kv"], done(i * BLOCKS + BLOCKS - 1))
                sp.dma_start(rows_of(kv_table, i), o14[:, :, :]).then_inc(s["out"], 16)
                sp.wait_ge(s["out"], i * 32 + 32)
                sp.sem_inc(s_past, 1)
            node_loop(stage0)

            def gather_lists(which, slots_idx):
                s = edge_sems[which]
                free = "msg" if which < 2 else "agg"
                with sp.Fori(0, EDGE_STEPS) as i:
                    for g in range(GROUPS):
                        n = i * GROUPS + g
                        sp.wait_ge(s[free], freed(n, RING))
                        sp.dma_start(idx_ring[:, g % RING, :], slots_idx[:, bass.ds(n * TILES, TILES)])\
                            .then_inc(s_idx[g % RING], 16)

            sp.wait_ge(sorts[0]["gidx"], 1)
            gather_lists(0, gidx)
            sp.wait_ge(edge_sems[0]["add"], CREDIT + NT)

            def stage1(i, last):
                s = node_sems[1]
                sp.dma_start(e14[:, :, :], rows_of(emb1_dram, i)).then_inc(s["e"], 16)
                sp.wait_ge(s["y"], i + 1)
                sp.dma_start(rows_of(emb2_dram, i), e14[:, :, :]).then_inc(s["out"], 16)
                sp.wait_ge(s["kv"], done(i * BLOCKS + BLOCKS - 1))
                sp.dma_start(rows_of(kv_table2, i), o14[:, :, :]).then_inc(s["out"], 16)
                sp.wait_ge(s["q"], done(i * BLOCKS + BLOCKS - 1))
                sp.wait_ge(s["out"], i * 32 + 32)
                sp.sem_inc(s_past, 1)
            node_loop(stage1)

            gather_lists(1, gidx)
            sp.wait_ge(edge_sems[1]["add"], CREDIT + NT)

            load_lists(1)

            def stage2(i, last):
                s = node_sems[2]
                sp.dma_start(e14[:, :, :], rows_of(emb2_dram, i)).then_inc(s["e"], 16)
                load_x(i, last, s["x"])
                sp.wait_ge(s["sum"], done(i * BLOCKS + BLOCKS - 1))
                sp.dma_start(rows_of(x1_dram, i), o14[:, :, :]).then_inc(s["out"], 16)
                sp.wait_ge(s["h"], done(i * BLOCKS + BLOCKS - 1))
                sp.dma_start(rows_of(h_table, i), x14[:, :, :]).then_inc(s["out"], 16)
                sp.wait_ge(s["out"], i * 32 + 32)
                sp.sem_inc(s_past, 1)
            node_loop(stage2)

            sp.wait_ge(sorts[1]["gidx"], 1)
            gather_lists(2, gidx)
            sp.wait_ge(edge_sems[2]["add"], CREDIT + NT)

            def stage3(i, last):
                s = node_sems[3]
                sp.dma_start(x14[:, :, :], rows_of(h_table, i)).then_inc(s["x"], 16)
                sp.dma_start(o14[:, :, :], rows_of(x1_dram, i)).then_inc(s["e"], 16)
                sp.wait_ge(s["sum"], done(i * BLOCKS + BLOCKS - 1))
                (w, _, a), (_, lanes, b) = ragged(i, last)
                sp.dma_start(out[a, :].rearrange("(b p) f -> p b f", p=P), o14[:, 0:w, :]).then_inc(s["out"], 16)
                sp.dma_start(out[b, :], o14[lanes, w, :]).then_inc(s["out"], 16)
                sp.wait_ge(s["out"], i * 32 + 32)
                sp.sem_inc(s_past, 1)
            node_loop(stage3)

        @block.gpsimd
        def _(pool):
            pool.iota(iota_n[:, :], pattern=[[1, P]], base=0, channel_multiplier=0,
                      allow_small_or_imprecise_dtypes=True).then_inc(s_const, 1)
            pool.iota(grid[:, :], pattern=[[1, GRID]], base=0, channel_multiplier=GRID,
                      allow_small_or_imprecise_dtypes=True).then_inc(s_const, 1)
            pool.memset(ident[:, :], 0.0).then_inc(s_const, 1)
            pool.memset(ones[:, :], 1.0).then_inc(s_const, 1)
            pool.memset(below[:, :], 1.0).then_inc(s_const, 1)
            pool.wait_ge(s_const, 5)
            pool.affine_select(out=ident[:, :], in_=ident[:, :], compare_op=ALU.not_equal, fill=1.0,
                               base=0, pattern=[[-1, P]], channel_multiplier=1).then_inc(s_const, 1)
            pool.affine_select(out=below[:, :], in_=below[:, :], compare_op=ALU.is_gt, fill=0.0,
                               base=0, pattern=[[1, P]], channel_multiplier=-1).then_inc(s_const, 1)
            pool.memset(q_sb[:, NB, :], 0.0).then_inc(s_const, 1)
            pool.memset(work[:, :], 0.0).then_inc(s_const, 1)

            def scatters(s, slots, width):
                pool.wait_ge(s["empty"], 16)
                with pool.Fori(0, STEPS) as i:
                    for par in range(2):
                        n = i * 2 + par
                        pool.wait_ge(s["pos"], done(n))
                        pool.wait_ge(s["rec"], done(n))
                        pool.sem_inc(s_past, 1)
                        for u in range(COLS):
                            pool.indirect_dma_start(
                                out=slots[:, :], out_offset=bass.IndirectOffsetOnAxis(ap=pos_ring[:, par, u:u + 1], axis=0),
                                in_=rec_ring[:, par, u, 0:width], in_offset=None).then_inc(s[f"out{par}"], 16)

            scatters(src_sort, slots_src, 2)
            pool.wait_ge(order["edges"], 16)
            pool.wait_ge(order["chunk"], 1)
            for j in range(GRID):
                pool.indirect_dma_start(
                    out=by_tile[:, j, :, :].rearrange("p e w -> p (e w)"), out_offset=None, in_=edge_rec[:, :],
                    in_offset=bass.IndirectOffsetOnAxis(ap=chunk[:, j:j + 1], axis=0)).then_inc(order["rows"], 16)
            pool.wait_ge(s_flag, 1)
            with pool.If(unordered(mybir.EngineType.Pool)):
                scatters(dst_sort, slots_dst, 3)
                for par in range(2):
                    pool.wait_ge(dst_sort[f"out{par}"], 16 * COLS * STEPS)

            def gathers(which, table):
                with pool.Fori(0, EDGE_STEPS) as i:
                    for g in range(GROUPS):
                        r = g % RING
                        pool.wait_ge(s_idx[r], idx_in(which, i, g))
                        pool.sem_inc(s_past, 1)
                        for u in range(TILES):
                            pool.indirect_dma_start(
                                out=rows[:, r, u, :], out_offset=None, in_=table[:, :],
                                in_offset=bass.IndirectOffsetOnAxis(ap=idx_ring[:, r, u:u + 1], axis=0)).then_inc(s_rows[r], 16)

            for which in range(3):
                s = edge_sems[which]
                if which == 0:
                    pool.wait_ge(order["slots"], 16)
                else:
                    pool.wait_ge(node_sems[which]["used"], NODE_STEPS)
                pool.memset((agg_sb if which < 2 else conv_sb)[:, :, :], 0.0).then_inc(s["clear"], 1)
                pool.wait_ge(node_sems[which]["out"], 32 * NODE_STEPS)
                gathers(which, (kv_table, kv_table2, h_table)[which])

        @block.scalar
        def _(act):
            for s in node_sems:
                give_credit(act, [s[k] for k in NODE_ACT if k in s])
            for s in edge_sems:
                give_credit(act, [s[k] for k in EDGE_ACT if k in s])
            for s in (src_sort, dst_sort):
                give_credit(act, [s["rec"]])
            act.wait_ge(s_const, 7)
            act.copy(ident16[:, :], ident[:, :]).then_inc(s_id16, 1)
            act.copy(iota16[:, :], iota_n[:, :]).then_inc(s_id16, 1)

            act.wait_ge(src_sort["in"], IN)
            act.copy(edges[:, :, 0], oth_int[:, :])
            act.copy(edges[:, :, 2], wgt[:, :]).then_inc(src_sort["edges"], 1)

            def records(s, recs, width):
                act.wait_ge(s["base"], 1)

                def step(i):
                    for par in range(2):
                        n = i * 2 + par
                        if not isinstance(i, int):
                            act.wait_ge(s[f"out{par}"], i * (16 * COLS))
                        act.copy(rec_ring[:, par, :, 0:width], recs[:, bass.ds(n * COLS, COLS), :]).then_inc(s["rec"], 1)
                step(0)
                with act.Fori(1, STEPS) as i:
                    step(i)

            records(src_sort, rec_src, 2)
            act.wait_ge(src_sort["loaded"], 16)
            act.copy(gidx[:, :], slot_src[:, :, 1]).then_inc(src_sort["gidx"], 1)
            for j in range(GRID):
                act.wait_ge(order["turned"], j + 1)
                act.copy(by_lane[:, j, :, :], pb[j % 2][:, 0:CHUNK].rearrange("p (w t) -> p t w", w=3)).then_inc(order["lanes"], 1)
            act.wait_ge(s_flag, 1)
            with act.If(unordered(mybir.EngineType.Activation)):
                for par in range(2):
                    act.wait_ge(src_sort[f"out{par}"], 16 * COLS * STEPS)
                records(dst_sort, rec_dst, 3)

            s = node_sems[0]
            act.wait_ge(sorts[0]["gidx"], 1)
            with act.Fori(0, NODE_STEPS) as i:
                act.wait_ge(s["st"], i + 1)
                act.activation(sd[:, :], sd[:, :], ACT.Sqrt).then_inc(s["sqrt"], 1)
                act.wait_ge(s["rs"], i + 1)
                for t in range(BLOCKS + 4):
                    j = t
                    if j < BLOCKS:
                        n = i * BLOCKS + j
                        act.wait_ge(s["hT_ps"], freed(n, 2))
                        act.activation(hs[:, j % 2, :], x14[:, j, :], ACT.Relu, bias=nb[:, j:j + 1],
                                       scale=rs[:, j:j + 1]).then_inc(s["h"], 1)
                    j = t - 3
                    if 0 <= j < BLOCKS:
                        n = i * BLOCKS + j
                        act.wait_ge(s["eT_ps"], done(n))
                        act.wait_ge(s["qkv"], freed(n, 2))
                        act.copy(eT[:, j % 2, :], pw[0][:, j % 2, 0:D]).then_inc(s["eT"], 1)
                    j = t - 4
                    if 0 <= j < BLOCKS:
                        n = i * BLOCKS + j
                        act.wait_ge(s["qkv"], done(n))
                        
                        act.copy(o14[:, j, :], pw[1][:, j % 2, D:3 * D]).then_inc(s["kv"], 1)

            def attention_act(which):
                s = edge_sems[which]
                with act.Fori(0, EDGE_STEPS) as i:
                    for t in range(GROUPS + 2):
                        g = t - 2
                        if 0 <= g < GROUPS:
                            n = i * GROUPS + g
                            act.wait_ge(s["clip"], done(n))
                            act.activation(msg[:, g % 2, :, D:MSG],
                                           score[:, g % 2, :].rearrange("p (t h) -> p t h", h=H), ACT.Exp)\
                                .then_inc(s["exp"], 1)
                        g = t
                        if g < GROUPS:
                            n = i * GROUPS + g
                            act.wait_ge(s["hot"], done(n))
                            act.copy(hot[:, g % HOTS, :, :], hot16[:, g % 2, :, :]).then_inc(s["hot32"], 1)
                            act.wait_ge(s["hotT_ps"], done(n))
                            if g >= 2:
                                act.wait_ge(s["q"], done(n - 2))
                            act.copy(hotT[:, g % 2, :], hotT_ps[g % 2]).then_inc(s["hotT"], 1)

            attention_act(0)
            s = node_sems[1]
            with act.Fori(0, NODE_STEPS) as i:
                act.wait_ge(s["st"], i + 1)
                act.activation(sd[:, :], sd[:, :], ACT.Sqrt).then_inc(s["sqrt"], 1)
                for t in range(BLOCKS + 1):
                    j = t
                    if j < BLOCKS:
                        n = i * BLOCKS + j
                        act.wait_ge(s["eT_ps"], done(n))
                        act.wait_ge(s["qkv"], freed(n, 2))
                        act.copy(eT[:, j % 2, :], pw[0][:, j % 2, 0:D]).then_inc(s["eT"], 1)
                    j = t - 1
                    if 0 <= j < BLOCKS:
                        n = i * BLOCKS + j
                        act.wait_ge(s["qkv"], done(n))
                        act.copy(o14[:, j, :], pw[1][:, j % 2, D:3 * D]).then_inc(s["kv"], 1)
            attention_act(1)
            act.wait_ge(sorts[1]["loaded"], 16)
            act.wait_ge(edge_sems[1]["add"], CREDIT + NT)
            act.copy(gidx[:, :], slot_dst[:, :, 1]).then_inc(sorts[1]["gidx"], 1)
            s = node_sems[2]
            with act.Fori(0, NODE_STEPS) as i:
                act.wait_ge(s["st"], 2 * i + 1)
                act.activation(sd[:, :], sd[:, :], ACT.Sqrt).then_inc(s["sqrt"], 1)
                for j in range(BLOCKS):
                    n = i * BLOCKS + j
                    act.wait_ge(s["eT_ps"], done(n))
                    act.wait_ge(s["qkv"], freed(n, 2))
                    act.copy(eT[:, j % 2, :], pw[0][:, j % 2, 0:D]).then_inc(s["eT"], 1)
                act.wait_ge(s["st"], 2 * i + 2)
                act.activation(sd[:, :], sd[:, :], ACT.Sqrt).then_inc(s["sqrt"], 1)
                act.wait_ge(s["rs"], i + 1)
                for j in range(BLOCKS):
                    n = i * BLOCKS + j
                    act.activation(x14[:, j, :], o14[:, j, :], ACT.Relu, bias=nb[:, j:j + 1],
                                   scale=rs[:, j:j + 1]).then_inc(s["h"], 1)
            s = node_sems[3]
            act.wait_ge(edge_sems[2]["add"], CREDIT + NT)
            with act.Fori(0, NODE_STEPS) as i:
                act.wait_ge(s["hT_ps"], i * BLOCKS + CREDIT)
                act.copy(c14[:, :, :], conv_sb[:, bass.ds(i * BLOCKS, BLOCKS), :]).then_inc(s["c"], 1)
                for j in range(BLOCKS):
                    n = i * BLOCKS + j
                    act.wait_ge(s["hT_ps"], done(n))
                    act.wait_ge(s["mm"], freed(n, 2))
                    act.copy(hsT[:, j % 2, :], pb[j % 2][:, :]).then_inc(s["eT"], 1)

        @block.tensor
        def _(pe):
            for s in node_sems:
                give_credit(pe, [s[k] for k in NODE_PE if k in s])
            for s in edge_sems:
                give_credit(pe, [s[k] for k in EDGE_PE if k in s])
            pe.wait_ge(s_const, 7)
            pe.wait_ge(s_id16, 1)
            pe.wait_ge(s_w, 16 * 18)

            pe.wait_ge(src_sort["cnt"], CREDIT + 1 + KC)
            nc.tensor.matmul(pb[1][:, 0:KB], below[:, :], cnt_src[:, 0:KB], start=True, stop=True)
            nc.tensor.matmul(pb[2][:, 0:KB], ones[:, :], cnt_src[:, 0:KB], start=True, stop=True)
            nc.tensor.matmul(pb[3][:, 0:2], ones[:, :], viol[:, :], start=True, stop=True).then_inc(src_sort["sums"], 1)
            pe.wait_ge(order["cnt"], CREDIT + KB)
            nc.tensor.matmul(pb[2][:, 0:KB], ones[:, :], cnt_dst[:, 0:KB], start=True, stop=True).then_inc(order["sums"], 1)
            for j in range(GRID):
                pe.wait_ge(order["node0"], j + 1)
                if j >= 2:
                    pe.wait_ge(order["lanes"], j - 1)
                for w in range(3):
                    last = nc.tensor.transpose(pb[j % 2][:, w * P:(w + 1) * P], by_tile[:, j, :, w], ident[:, :])
                last.then_inc(order["turned"], 1)
            pe.wait_ge(s_flag, 1)
            with pe.If(unordered(mybir.EngineType.PE)):
                pe.wait_ge(order["lanes"], GRID)
                nc.tensor.matmul(pb[1][:, 0:KB], below[:, :], cnt_dst[:, 0:KB], start=True, stop=True)
                nc.tensor.matmul(pb[2][:, 0:KB], ones[:, :], cnt_dst[:, 0:KB], start=True, stop=True)\
                    .then_inc(dst_sort["sums"], 1)

            def qkv_steps(i, s, w, t):
                j = t
                if 0 <= j < BLOCKS:
                    n = i * BLOCKS + j
                    pe.wait_ge(s["eT"], freed(n, 2))
                    nc.tensor.transpose(pw[0][:, j % 2, 0:D], e14[:, j, :], ident[:, :]).then_inc(s["eT_ps"], 1)
                j = t - 1
                if 0 <= j < BLOCKS:
                    n = i * BLOCKS + j
                    pe.wait_ge(s["eT"], done(n))
                    pe.wait_ge(s["q"], freed(n, 2))
                    pe.wait_ge(s["kv"], freed(n, 2))
                    nc.tensor.matmul(pw[1][:, j % 2, 0:3 * D], eT[:, j % 2, :], w[:, :], start=True, stop=True)\
                        .then_inc(s["qkv"], 1)

            s = node_sems[0]
            with pe.Fori(0, NODE_STEPS) as i:
                for t in range(BLOCKS + 4):
                    j = t
                    if j < BLOCKS:
                        n = i * BLOCKS + j
                        pe.wait_ge(s["h"], done(n))
                        pe.wait_ge(s["hT"], freed(n, 2))
                        nc.tensor.transpose(pb[j % 2][:, 0:P], hs[:, j % 2, 0:P], ident[:, :])
                        nc.tensor.transpose(pb[j % 2][:, P:2 * P], hs[:, j % 2, P:2 * P], ident[:, :])\
                            .then_inc(s["hT_ps"], 1)
                    j = t - 1
                    if 0 <= j < BLOCKS:
                        n = i * BLOCKS + j
                        pe.wait_ge(s["hT"], done(n))
                        pe.wait_ge(s["emb"], freed(n, 2))
                        nc.tensor.matmul(pb[2 + j % 2][:, 0:D], hsT[:, j % 2, 0:P], wp[:, 0, :], start=True, stop=False)
                        nc.tensor.matmul(pb[2 + j % 2][:, 0:D], hsT[:, j % 2, P:2 * P], wp[:, 1, :], start=False,
                                         stop=True).then_inc(s["mm"], 1)
                    if 0 <= t - 2 < BLOCKS:
                        pe.wait_ge(s["emb"], done(i * BLOCKS + t - 2))
                    qkv_steps(i, s, wqkv1, t - 2)

            def attention_pe(which):
                s = edge_sems[which]
                pe.wait_ge(s["clear"], 1)
                with pe.Fori(0, EDGE_STEPS) as i:
                    for t in range(GROUPS + 3):
                        if t < GROUPS:
                            g = t
                            n = i * GROUPS + g
                            pe.wait_ge(s["hot"], done(n))
                            for u in range(TILES):
                                last = nc.tensor.transpose(hotT_ps[g % 2][:, u * P:(u + 1) * P],
                                                           hot16[:, g % 2, u, :], ident16[:, :])
                            last.then_inc(s["hotT_ps"], 1)
                        g = t - 3
                        if g >= 0:
                            n = i * GROUPS + g
                            pe.wait_ge(s["msg"], done(n))
                            for u in range(TILES):
                                last = nc.tensor.matmul(pw4(g % 2)[:, u, 0:MSG], hot[:, g % HOTS, u, :],
                                                        msg[:, g % 2, u, :], start=True, stop=True)
                            last.then_inc(s["agg"], 1)
                        if t < GROUPS:
                            g = t
                            n = i * GROUPS + g
                            blks = tile_blocks(mybir.EngineType.PE, n)
                            pe.wait_ge(s["hotT"], done(n))
                            if g >= 2:
                                pe.wait_ge(s["prod"], done(n - 2))
                            for u in range(TILES):
                                last = nc.tensor.matmul(pb[2 + g % 2][:, u * P:(u + 1) * P],
                                                        hotT[:, g % 2, u * P:(u + 1) * P],
                                                        q_sb[:, bass.ds(blks[u], 1), :], start=True, stop=True)
                            last.then_inc(s["q"], 1)

            pe.wait_ge(sorts[0]["row"], 32)
            attention_pe(0)
            s = node_sems[1]
            with pe.Fori(0, NODE_STEPS) as i:
                pe.wait_ge(s["y"], i + 1)
                for t in range(BLOCKS + 1):
                    qkv_steps(i, s, wqkv2, t)
            attention_pe(1)
            s = node_sems[2]
            with pe.Fori(0, NODE_STEPS) as i:
                pe.wait_ge(s["y"], i + 1)
                for t in range(BLOCKS + 1):
                    j = t
                    if j < BLOCKS:
                        n = i * BLOCKS + j
                        pe.wait_ge(s["eT"], freed(n, 2))
                        nc.tensor.transpose(pw[0][:, j % 2, 0:D], e14[:, j, :], ident[:, :]).then_inc(s["eT_ps"], 1)
                    j = t - 1
                    if j >= 0:
                        n = i * BLOCKS + j
                        pe.wait_ge(s["eT"], done(n))
                        pe.wait_ge(s["sum"], freed(n, 2))
                        nc.tensor.matmul(pw[1][:, j % 2, 0:F], eT[:, j % 2, :], winv[:, :], start=True, stop=True)\
                            .then_inc(s["qkv"], 1)
            s = edge_sems[2]
            pe.wait_ge(s["clear"], 1)
            with pe.Fori(0, EDGE_STEPS) as i:
                for g in range(GROUPS):
                    n = i * GROUPS + g
                    pe.wait_ge(s["hot"], done(n))
                    pe.wait_ge(s_rows[g % RING], rows_in(2, i, g))
                    if g >= 2:
                        pe.wait_ge(s["add"], n * TILES + (CREDIT - TILES))
                    for u in range(TILES):
                        last = nc.tensor.matmul(pw4(g % 2)[:, u, :], hot[:, g % HOTS, u, :], rows[:, g % RING, u, :],
                                                start=True, stop=True)
                    last.then_inc(s["agg"], 1)
            s = node_sems[3]
            with pe.Fori(0, NODE_STEPS) as i:
                pe.wait_ge(s["x"], (i + 1) * 16)
                pe.wait_ge(s["c"], i + 1)
                for t in range(BLOCKS + 1):
                    j = t
                    if j < BLOCKS:
                        n = i * BLOCKS + j
                        pe.wait_ge(s["eT"], freed(n, 2))
                        for k in range(2):
                            nc.tensor.transpose(pb[j % 2][:, k * P:(k + 1) * P],
                                                c14[:, j, k * P:(k + 1) * P], ident[:, :])
                        for k in range(2):
                            last = nc.tensor.transpose(pb[j % 2][:, (2 + k) * P:(3 + k) * P],
                                                       x14[:, j, k * P:(k + 1) * P], ident[:, :])
                        last.then_inc(s["hT_ps"], 1)
                    j = t - 1
                    if j >= 0:
                        n = i * BLOCKS + j
                        pe.wait_ge(s["eT"], done(n))
                        pe.wait_ge(s["sum"], freed(n, 2))
                        for k in range(4):
                            w = (wn if k < 2 else wo)[:, k % 2, :]
                            last = nc.tensor.matmul(pb[2 + j % 2][:, 0:F], hsT[:, j % 2, k * P:(k + 1) * P], w,
                                                    start=(k == 0), stop=(k == 3))
                        last.then_inc(s["mm"], 1)

        @block.vector
        def _(dve):
            V = nc.vector
            for s in node_sems:
                give_credit(dve, [s[k] for k in NODE_DVE if k in s])
            for s in edge_sems:
                give_credit(dve, [s[k] for k in EDGE_DVE if k in s])
            give_credit(dve, [src_sort["pos"], dst_sort["pos"], src_sort["cnt"], order["cnt"]])

            def chain_of(s):
                count = [0]

                def link(ins):
                    count[0] += 1
                    ins.then_inc(s["link"], 1)
                    dve.wait_ge(s["link"], count[0])
                return link

            def shifted(link, to, value):
                link(V.tensor_copy(tot_i[:, :], value))
                link(V.tensor_scalar(tot_i[:, :], tot_i[:, :], 7, None, ALU.arith_shift_right))
                link(V.tensor_copy(to[:, :], tot_i[:, :]))

            def tile_table(link, s):
                for j in range(GRID):
                    link(V.tensor_scalar(junk[:, :], tend[:, :], grid[:, j:j + 1], 0.0, ALU.is_le, ALU.add,
                                         accum_out=blk_f[:, j:j + 1]))
                link(V.tensor_scalar(blk_f[:, :], blk_f[:, :], float(NB), None, ALU.min))
                link(V.tensor_copy(blk_i[:, :], blk_f[:, :]))
                dve.sem_inc(s["brow"], 1)

            def slot_table(link, s):
                link(V.tensor_scalar(tot[:, :], pb[2][:, 0:KB], float(P - 1), None, ALU.add))
                shifted(link, ntile, tot[:, :])
                link(V.tensor_tensor_scan(tend[:, :], ones[:, 0:KB], ntile[:, :], 0.0, ALU.mult, ALU.add))
                link(V.tensor_tensor(nxt[:, :], tend[:, :], ntile[:, :], ALU.subtract))
                link(V.scalar_tensor_tensor(nxt[:, :], nxt[:, :], float(P), pb[1][:, 0:KB], ALU.mult, ALU.add))
                tile_table(link, s)
                dve.sem_inc(s["base"], 1)

            def count_dst(n):
                dve.wait_ge(order["cnt"], freed(n, 1))
                V.tensor_scalar(junk16[:, 0, :], dst16[:, :], iota_n[:, bass.ds(n, 1)], 0.0, ALU.is_equal, ALU.add,
                                accum_out=cnt_dst[:, bass.ds(n, 1)]).then_inc(order["cnt"], 1)

            def positions(s, with_count):
                dve.sem_inc(s["chain"], 1)

                def step(i):
                    for par in range(2):
                        n = i * 2 + par
                        for u in range(COLS):
                            kb = key_blk[:, bass.ds(n * COLS + u, 1)]
                            dve.wait_ge(s["chain"], n * COLS + u + 1)
                            V.scalar_tensor_tensor(junk[:, :], iota_n[:, 0:KB], kb, nxt[:, :], ALU.is_equal,
                                                   ALU.mult, accum_out=slot_f[:, u:u + 1])
                            V.scalar_tensor_tensor(nxt[:, :], iota_n[:, 0:KB], kb, nxt[:, :], ALU.is_equal,
                                                   ALU.add).then_inc(s["chain"], 1)
                        dve.wait_ge(s["chain"], n * COLS + COLS + 1)
                        V.tensor_copy(slot_i[:, :], slot_f[:, :]).then_inc(s["conv"], 1)
                        dve.wait_ge(s["conv"], n * 3 + 1)
                        V.tensor_scalar(lane_i[:, :], slot_i[:, :], P - 1, None, ALU.bitwise_and)
                        V.tensor_scalar(tile_i[:, :], slot_i[:, :], 7, None, ALU.arith_shift_right).then_inc(s["conv"], 1)
                        dve.wait_ge(s["conv"], n * 3 + 2)
                        V.tensor_copy(lane_f[:, :], lane_i[:, :])
                        V.tensor_copy(tile_f[:, :], tile_i[:, :]).then_inc(s["conv"], 1)
                        dve.wait_ge(s["conv"], n * 3 + 3)
                        if not isinstance(i, int):
                            dve.wait_ge(s[f"out{par}"], i * (16 * COLS))
                        V.scalar_tensor_tensor(pos_ring[:, par, :], lane_f[:, :], float(NT), tile_f[:, :], ALU.mult,
                                               ALU.add).then_inc(s["pos"], 1)
                    if with_count:
                        count_dst(i)
                step(0)
                with dve.Fori(1, STEPS) as i:
                    step(i)

            s = src_sort
            link = chain_of(s)
            link(V.memset(key_int[96:P, :], NB * P))
            link(V.memset(oth_int[96:P, :], NB * P))
            link(V.memset(wgt[96:P, :], 0.0))
            link(V.memset(next_int[:, :], NB * P))
            dve.sem_inc(s["keys"], 1)
            link(V.memset(empty_src[:, :, 0], -1.0))
            link(V.memset(empty_src[:, :, 1], 0.0))
            dve.sem_inc(s["empty_ms"], 1)
            dve.wait_ge(s["in"], IN)
            link(V.tensor_scalar(blk_int[:, :], key_int[:, :], 7, None, ALU.arith_shift_right))
            link(V.tensor_copy(key16[:, :], blk_int[:, :]))
            dve.wait_ge(s_const, 9)
            with dve.Fori(0, KC // 2) as i:
                for par in range(2):
                    n = i * 2 + par
                    dve.wait_ge(s["cnt"], freed(n, 2))
                    V.tensor_scalar(junk16[:, par, :], key16[:, :], iota_n[:, bass.ds(n, 1)], 0.0, ALU.is_equal, ALU.add,
                                    accum_out=cnt_src[:, bass.ds(n, 1)]).then_inc(s["cnt"], 1)
            dve.wait_ge(s["edges"], 1)
            link(V.tensor_tensor(descents[:, 0:C - 1], edges[:, 0:C - 1, 0], edges[:, 1:C, 0], ALU.is_gt))
            link(V.tensor_reduce(viol[:, 0:1], descents[:, 0:C - 1], AX.X, ALU.add))
            link(V.tensor_copy(next_f[:, :], next_int[:, :]))
            link(V.tensor_tensor(viol[:, 1:2], edges[:, C - 1, 0:1], next_f[:, :], ALU.is_gt))
            dve.sem_inc(s["cnt"], 1)
            link(V.tensor_copy(key_blk[:, :], blk_int[:, :]))
            link(V.tensor_copy(rec_src[:, :, 0], key_int[:, :]))
            link(V.scalar_tensor_tensor(rec_src[:, :, 0], key_blk[:, :], -float(P), rec_src[:, :, 0], ALU.mult, ALU.add))
            link(V.tensor_scalar(rec_src[:, :, 1], oth_int[:, :], 0, N - 1, ALU.max, ALU.min))
            link(V.tensor_scalar(edges[:, :, 1], key_int[:, :], 0, N - 1, ALU.max, ALU.min))
            dve.sem_inc(s["edges"], 1)
            link(V.tensor_scalar(blk_int[:, :], oth_int[:, :], 7, None, ALU.arith_shift_right))
            link(V.tensor_copy(dst16[:, :], blk_int[:, :]))
            dve.wait_ge(s["sums"], 1)
            link(V.tensor_copy(flag_f[:, :], pb[3][:, 0:1]))
            link(V.tensor_tensor(flag_f[:, :], flag_f[:, :], pb[3][:, 1:2], ALU.add))
            link(V.tensor_scalar(flag[:, :], flag_f[:, :], 1.0, None, ALU.min))
            dve.sem_inc(s_flag, 1)
            slot_table(link, s)
            positions(s, True)
            for n in range(STEPS, KB):
                count_dst(n)

            s = order
            link = chain_of(s)
            dve.wait_ge(s["sums"], 1)
            dve.wait_ge(src_sort["row"], 16)
            link(V.tensor_copy(tot[:, :], pb[2][:, 0:KB]))
            link(V.tensor_tensor_scan(end[:, :], ones[:, 0:KB], tot[:, :], 0.0, ALU.mult, ALU.add))
            shifted(link, c_end, end[:, :])
            link(V.tensor_tensor(c_start[:, :], end[:, :], tot[:, :], ALU.subtract))
            shifted(link, c_start, c_start[:, :])
            link(V.tensor_scalar(c_stop[:, :], end[:, :], float(P - 1), None, ALU.add))
            shifted(link, c_stop, c_stop[:, :])
            link(V.tensor_tensor(c_stop[:, :], c_stop[:, :], c_start[:, :], ALU.subtract))
            link(V.scalar_tensor_tensor(ntile[:, :], tot[:, :], 0.0, c_stop[:, :], ALU.is_gt, ALU.mult))
            link(V.tensor_tensor_scan(tend[:, :], ones[:, 0:KB], ntile[:, :], 0.0, ALU.mult, ALU.add))
            link(V.tensor_tensor(shift[:, :], c_end[:, :], c_start[:, :], ALU.subtract))
            link(V.tensor_tensor(shift[:, :], shift[:, :], ntile[:, :], ALU.subtract))
            for j in range(GRID):
                link(V.scalar_tensor_tensor(junk[:, :], tend[:, :], grid[:, j:j + 1], shift[:, :], ALU.is_le, ALU.mult,
                                            accum_out=chunk_f[:, j:j + 1]))
            link(V.tensor_tensor(chunk_f[:, :], chunk_f[:, :], grid[:, :], ALU.add))
            link(V.tensor_scalar(chunk[:, :], chunk_f[:, :], float(C - 1), None, ALU.min))
            dve.sem_inc(s["chunk"], 1)
            tile_table(link, s)
            link(V.tensor_scalar(node0[:, :], blk_f[:, :], -float(P), None, ALU.mult))
            dve.wait_ge(s["rows"], 16 * GRID)
            for j in range(GRID):
                V.tensor_scalar(by_tile[:, j, :, 0], by_tile[:, j, :, 0], node0[:, j:j + 1], None, ALU.add)\
                    .then_inc(s["node0"], 1)
            with dve.If(unordered(mybir.EngineType.DVE)):
                s = dst_sort
                link = chain_of(s)
                dve.wait_ge(order["row"], 16)
                dve.wait_ge(s["in"], 16)
                link(V.tensor_copy(dblk_int[:, :], rec_dst[:, :, 0]))
                link(V.tensor_scalar(dblk_int[:, :], dblk_int[:, :], 7, None, ALU.arith_shift_right))
                link(V.tensor_copy(key_blk[:, :], dblk_int[:, :]))
                link(V.scalar_tensor_tensor(rec_dst[:, :, 0], key_blk[:, :], -float(P), rec_dst[:, :, 0], ALU.mult, ALU.add))
                link(V.memset(empty_dst[:, :, 0], -1.0))
                link(V.memset(empty_dst[:, :, 1:3], 0.0))
                dve.sem_inc(s["empty_ms"], 1)
                dve.wait_ge(s["sums"], 1)
                slot_table(link, s)
                positions(s, False)

            def normalise(src14, eps, s, k, turn, i, lanes=1):
                base = turn * 4
                for j in range(BLOCKS):
                    last = V.bn_stats(st6[:, j, :], src14[:, j, :])
                last.then_inc(s["part"], 1)
                dve.wait_ge(s["part"], base + 1)
                dve.sem_inc(s_past, 1)
                for j in range(BLOCKS):
                    last = V.bn_aggr(mv[:, j, :], st6[:, j, :])
                last.then_inc(s["part"], 1)
                dve.wait_ge(s["part"], base + 2)
                V.tensor_scalar(sd[:, :], mv[:, :, 1], eps, None, ALU.add).then_inc(s["st"], 1)
                dve.wait_ge(s["sqrt"], turn + 1)
                V.reciprocal(rs[:, :], sd[:, :]).then_inc(s["part"], 1)
                dve.wait_ge(s["part"], base + 3)
                V.scalar_tensor_tensor(nb[:, :], mv[:, :, 0], -1.0, rs[:, :], ALU.mult, ALU.mult).then_inc(s["part"], 1)
                dve.wait_ge(s["part"], base + 4)

            s = node_sems[0]
            dve.wait_ge(s_w, 16 * 18)
            V.tensor_tensor(pbias[:, 0, :], pbias[:, 0, :], pbias[:, 1, :], ALU.add).then_inc(s["link"], 1)
            dve.wait_ge(s["link"], 1)
            with dve.Fori(0, NODE_STEPS) as i:
                dve.wait_ge(s["x"], i * 32 + 32)
                normalise(x14, EPS, s, 0, i, i)
                dve.sem_inc(s["rs"], 1)
                for t in range(BLOCKS + 4):
                    j = t
                    if j < BLOCKS:
                        n = i * BLOCKS + j
                        dve.wait_ge(s["hT_ps"], done(n))
                        dve.wait_ge(s["mm"], freed(n, 2))
                        V.tensor_copy(hsT[:, j % 2, 0:2 * P], pb[j % 2][:, 0:2 * P]).then_inc(s["hT"], 1)
                    j = t - 1
                    if 0 <= j < BLOCKS:
                        n = i * BLOCKS + j
                        dve.wait_ge(s["mm"], done(n))
                        V.tensor_tensor(e14[:, j, :], pb[2 + j % 2][:, 0:D], pbias[:, 0, :], ALU.add).then_inc(s["emb"], 1)
                    j = t - 4
                    if 0 <= j < BLOCKS:
                        n = i * BLOCKS + j
                        dve.wait_ge(s["kv"], done(n))
                        V.tensor_copy(q_sb[:, bass.ds(n, 1), :], pw[1][:, j % 2, 0:D].unsqueeze(1)).then_inc(s["q"], 1)

            def add_tile(s, n, u, buf, blk, to, width):
                if u == 0:
                    dve.wait_ge(s["agg"], done(n))
                dve.wait_ge(s["add"], n * TILES + (u + CREDIT))
                last = V.tensor_tensor(to[:, bass.ds(blk, 1), :], to[:, bass.ds(blk, 1), :],
                                       pw4(buf)[:, u:u + 1, 0:width], ALU.add)
                last.then_inc(s["add"], 1)

            def attention(which):
                s = edge_sems[which]
                dve.wait_ge(node_sems[which]["out"], 32 * NODE_STEPS)
                dve.wait_ge(s["clear"], 1)
                with dve.Fori(0, EDGE_STEPS) as i:
                    for t in range(GROUPS + 4):
                        a, b, c = t, t - 2, t - 4
                        hots, scores, sums = a < GROUPS, 0 <= b < GROUPS, c >= 0
                        na, n, nc_ = i * GROUPS + a, i * GROUPS + b, i * GROUPS + c
                        if sums:
                            blks = tile_blocks(mybir.EngineType.DVE, nc_)
                        r = b % RING
                        if scores:
                            dve.wait_ge(s["q"], done(n))
                            dve.wait_ge(s_rows[r], rows_in(which, i, b))
                            V.tensor_tensor(prod.rearrange("p (t d) -> p t d", t=TILES),
                                            pb[2 + b % 2][:, :].rearrange("p (t d) -> p t d", t=TILES),
                                            rows[:, r, :, 0:D], ALU.mult).then_inc(s["prod"], 1)
                        if sums:
                            add_tile(s, nc_, 0, c % 2, blks[0], agg_sb, MSG)
                        if scores:
                            dve.wait_ge(s["prod"], done(n))
                            V.tensor_reduce(score[:, b % 2, :], prod.rearrange("p (h d) -> p h d", d=HD),
                                            AX.X, ALU.add).then_inc(s["score"], 1)
                        if sums:
                            add_tile(s, nc_, 1, c % 2, blks[1], agg_sb, MSG)
                        if scores:
                            dve.wait_ge(s["score"], done(n))
                            V.tensor_scalar(score[:, b % 2, :], score[:, b % 2, :], 10.0, -10.0, ALU.min, ALU.max)\
                                .then_inc(s["clip"], 1)
                        if hots:
                            for u in range(TILES):
                                last = V.tensor_scalar(hot16[:, a % 2, u, :], iota16[:, :],
                                                       slot_src[:, bass.ds(na * TILES + u, 1), 0], None,
                                                       ALU.is_equal)
                            last.then_inc(s["hot"], 1)
                        if sums:
                            add_tile(s, nc_, 2, c % 2, blks[2], agg_sb, MSG)
                            add_tile(s, nc_, 3, c % 2, blks[3], agg_sb, MSG)
                        if scores:
                            dve.wait_ge(s["exp"], done(n))
                            V.tensor_tensor(msg[:, b % 2, :, 0:D].rearrange("p t (h d) -> p t h d", d=HD),
                                            rows[:, r, :, D:2 * D].rearrange("p t (h d) -> p t h d", d=HD),
                                            msg[:, b % 2, :, D:MSG].unsqueeze(3).to_broadcast([P, TILES, H, HD]),
                                            ALU.mult).then_inc(s["msg"], 1)

            def layer_out(s, layer, i):
                count = [0]
                LINKS = 7

                def link(ins):
                    count[0] += 1
                    ins.then_inc(s["link"], 1)
                    dve.wait_ge(s["link"], i * LINKS + count[0])

                step = bass.ds(i * BLOCKS, BLOCKS)
                heads = [P, BLOCKS, H, HD]
                link(V.tensor_scalar(rnorm[:, :, :], agg_sb[:, step, D:MSG], 1e-8, None, ALU.add))
                link(V.reciprocal(rnorm[:, :, :], rnorm[:, :, :]))
                link(V.tensor_tensor(y14[:, :, :].rearrange("p b (h d) -> p b h d", d=HD),
                                     agg_sb[:, step, 0:D].rearrange("p b (h d) -> p b h d", d=HD),
                                     rnorm[:, :, :].unsqueeze(3).to_broadcast(heads), ALU.mult))
                dve.sem_inc(s["used"], 1)
                link(V.tensor_tensor(y14[:, :, :], y14[:, :, :], e14[:, :, :], ALU.add))
                normalise(y14, 1e-6, s, 0, i * (1 + layer), i)
                for j in range(BLOCKS):
                    last = V.tensor_scalar(y14[:, j, :], y14[:, j, :], rs[:, j:j + 1], nb[:, j:j + 1], ALU.mult, ALU.add)
                link(last)
                rowb = [P, BLOCKS, D]
                link(V.tensor_tensor(e14[:, :, :], y14[:, :, :], lns[:, layer, 0, :].unsqueeze(1).to_broadcast(rowb),
                                     ALU.mult))
                link(V.tensor_tensor(e14[:, :, :], e14[:, :, :], lns[:, layer, 1, :].unsqueeze(1).to_broadcast(rowb),
                                     ALU.add))
                assert count[0] == LINKS
                dve.sem_inc(s["y"], 1)

            dve.wait_ge(src_sort["row"], 32)
            attention(0)
            s = node_sems[1]
            with dve.Fori(0, NODE_STEPS) as i:
                dve.wait_ge(s["e"], i * 16 + 16)
                layer_out(s, 0, i)
                for j in range(BLOCKS):
                    n = i * BLOCKS + j
                    dve.wait_ge(s["kv"], done(n))
                    V.tensor_copy(q_sb[:, bass.ds(n, 1), :], pw[1][:, j % 2, 0:D].unsqueeze(1)).then_inc(s["q"], 1)
            attention(1)
            s = node_sems[2]
            with dve.Fori(0, NODE_STEPS) as i:
                dve.wait_ge(s["e"], i * 16 + 16)
                dve.wait_ge(s["x"], i * 32 + 32)
                layer_out(s, 1, i)
                for j in range(BLOCKS):
                    n = i * BLOCKS + j
                    dve.wait_ge(s["qkv"], done(n))
                    V.tensor_tensor(o14[:, j, :], pw[1][:, j % 2, 0:F], invb[:, :], ALU.add).then_inc(s["q"], 1)
                    dve.wait_ge(s["q"], done(n))
                    V.tensor_tensor(o14[:, j, :], o14[:, j, :], x14[:, j, :], ALU.add).then_inc(s["sum"], 1)
                dve.wait_ge(s["sum"], done(i * BLOCKS + BLOCKS - 1))
                normalise(o14, EPS, s, 0, i * 2 + 1, i)
                dve.sem_inc(s["rs"], 1)
            s = edge_sems[2]
            dve.wait_ge(sorts[1]["row"], 32)
            dve.wait_ge(node_sems[2]["out"], 32 * NODE_STEPS)
            dve.wait_ge(s["clear"], 1)
            with dve.Fori(0, EDGE_STEPS) as i:
                for t in range(GROUPS + 2):
                    a, c = t, t - 2
                    na, nc_ = i * GROUPS + a, i * GROUPS + c
                    if c >= 0:
                        blks = tile_blocks(mybir.EngineType.DVE, nc_)
                    for u in range(TILES):
                        if c >= 0:
                            add_tile(s, nc_, u, c % 2, blks[u], conv_sb, F)
                        if a < GROUPS:
                            at = bass.ds(na * TILES + u, 1)
                            last = V.tensor_scalar(hot[:, a % HOTS, u, :], iota_n[:, :], slot_dst[:, at, 0],
                                                   slot_dst[:, at, 2], ALU.is_equal, ALU.mult)
                            if u == TILES - 1:
                                last.then_inc(s["hot"], 1)
            s = node_sems[3]
            with dve.Fori(0, NODE_STEPS) as i:
                dve.wait_ge(s["e"], i * 16 + 16)
                for j in range(BLOCKS):
                    n = i * BLOCKS + j
                    dve.wait_ge(s["mm"], done(n))
                    V.tensor_tensor(o14[:, j, :], pb[2 + j % 2][:, 0:F], o14[:, j, :], ALU.add).then_inc(s["q"], 1)
                    dve.wait_ge(s["q"], done(n))
                    V.tensor_tensor(o14[:, j, :], o14[:, j, :], cbias[:, :], ALU.add).then_inc(s["sum"], 1)


_INS = ['x', 'src', 'dst', 'edge_weight', 'L0_gnn_W_P_w', 'L0_gnn_W_P_b', 'L0_gnn_W_pos', 'L0_gnn_q1', 'L0_gnn_k1',
        'L0_gnn_v1', 'L0_gnn_ln1_s', 'L0_gnn_ln1_b', 'L0_gnn_q2', 'L0_gnn_k2', 'L0_gnn_v2', 'L0_gnn_ln2_s',
        'L0_gnn_ln2_b', 'L0_gnn_inv_w', 'L0_gnn_inv_b', 'L1_gnn_w_nbr', 'L1_gnn_w_own', 'L1_gnn_bias']


def kernel(**inputs):
    import numpy as _np
    import concourse.bacc as _bacc
    from concourse import mybir as _mybir
    from concourse.bass_utils import run_bass_kernel_spmd as _run

    nc = _bacc.Bacc("TRN2", target_bir_lowering=False, num_devices=1)
    arrays, args = {}, []
    for name in _INS:
        a = _np.ascontiguousarray(inputs[name])
        arrays[f"in_{name}_dram"] = a
        args.append(nc.dram_tensor(f"in_{name}_dram", a.shape, _mybir.dt.from_np(a.dtype), kind="ExternalInput").ap())
    shape = tuple(inputs["x"].shape)
    args.append(nc.dram_tensor("out_0_dram", shape, _mybir.dt.float32, kind="ExternalOutput").ap())
    gnn_kernel(nc, *args)
    r = _run(nc, [arrays], core_ids=[0])
    return r.results[0]["out_0_dram"]
```
